# Optimizing a Trainium2 kernel written in Bass

```python
import numpy as np
import jax
import jax.numpy as jnp

def _softmax(x, axis=-1):
    return jax.nn.softmax(x, axis=axis)

def _gelu(x):
    return jax.nn.gelu(x, approximate=True)

def _silu(x):
    return jax.nn.silu(x)

def _sigmoid(x):
    return jax.nn.sigmoid(x)

def _layernorm(x, axis=-1, eps=1e-05):
    m = jnp.mean(x, axis=axis, keepdims=True)
    v = jnp.var(x, axis=axis, keepdims=True)
    return (x - m) / jnp.sqrt(v + eps)

def _scatter_add(tgt, idx, src, axis=0):
    return tgt.at[idx].add(src)

def _segment_sum(src, seg, n):
    return jax.ops.segment_sum(src, seg, n)
kernel_name = 'mk_gps_d1_gnn_r8_f9cb1d'

def setup_inputs(seed: int=0):
    np.random.seed(seed)
    _w = jnp.asarray

    def _rec_inputs():
        import jax
        import jax.numpy as jnp
        _gk = jax.random.key(seed)
        x = -6.415e-05 + 1 * jax.random.normal(jax.random.fold_in(_gk, 1), (1250, 1024), jnp.float32)
        src = jax.random.randint(jax.random.fold_in(_gk, 2), (40000,), 0, 1250, jnp.int32)
        dst = jnp.minimum((1250 * jax.random.uniform(jax.random.fold_in(_gk, 3), (40000,)) ** 2.0).astype(jnp.int32), 9999)
        _o = jnp.argsort(dst, stable=True)
        src = src[_o]
        dst = dst[_o]
        return (x, src, dst)
    x, src, dst = _rec_inputs()

    def _L0_gnn_setup():
        import jax, jax.numpy as jnp
        import numpy as np
        N_NODES = 1250
        N_EDGES = 20000
        DIM = 1024
        key = jax.random.key(seed)
        k1, k2, k3 = jax.random.split(key, 3)
        x = jax.random.normal(k1, (N_NODES, DIM), dtype=jnp.float32)
        edge_index = jax.random.randint(k2, (2, N_EDGES), 0, N_NODES, dtype=jnp.int64)
        W = jax.random.normal(k3, (DIM, DIM), dtype=jnp.float32) * (1.0 / np.sqrt(DIM))
        b = jnp.zeros((DIM,), dtype=jnp.float32)
        return {'x': x, 'edge_index': edge_index, 'W': W, 'b': b}
    _L0_gnn_all = _L0_gnn_setup()
    _L0_gnn_in = {k: v for k, v in _L0_gnn_all.items() if k in ('W', 'b')}
    del _L0_gnn_all

    def _L0_mix_setup():
        import jax, jax.numpy as jnp
        import numpy as np
        B, L, D = (2, 256, 1024)
        H = 16
        DH = D // H
        key = jax.random.key(seed)
        ks = jax.random.split(key, 9)
        s = 1.0 / np.sqrt(D)
        return {'x': jax.random.normal(ks[0], (B, L, D), dtype=jnp.float32), 'Wq': jax.random.normal(ks[1], (D, D), dtype=jnp.float32) * s, 'bq': jnp.zeros((D,), dtype=jnp.float32), 'Wk': jax.random.normal(ks[2], (D, D), dtype=jnp.float32) * s, 'bk': jnp.zeros((D,), dtype=jnp.float32), 'Wv': jax.random.normal(ks[3], (D, D), dtype=jnp.float32) * s, 'bv': jnp.zeros((D,), dtype=jnp.float32), 'Wo': jax.random.normal(ks[4], (D, D), dtype=jnp.float32) * s, 'bo': jnp.zeros((D,), dtype=jnp.float32)}
    _L0_mix_all = _L0_mix_setup()
    _L0_mix_in = {k: v for k, v in _L0_mix_all.items() if k in ('Wq', 'bq', 'Wk', 'bk', 'Wv', 'bv', 'Wo', 'bo')}
    del _L0_mix_all

    def _L0_ffn_setup():
        import jax, jax.numpy as jnp
        import numpy as np
        QMAX = 127.0

        def _ste_round(v):
            return v + jax.lax.stop_gradient(jnp.round(v) - v)

        def _act_fake_quant(x, clip_factor):
            scale = jax.nn.sigmoid(clip_factor) * jnp.max(jnp.abs(x)) / QMAX
            return jnp.clip(_ste_round(x / scale), -QMAX - 1.0, QMAX) * scale

        def _weight_fake_quant(w):
            scale = jnp.max(jnp.abs(w), axis=1, keepdims=True) / QMAX
            return jnp.clip(_ste_round(w / scale), -QMAX - 1.0, QMAX) * scale
        key = jax.random.key(seed)
        k1, k2, k3, k4 = jax.random.split(key, 4)
        B, S, H, I = (8, 1024, 1024, 352)
        return {'x': jax.random.normal(k1, (B, S, H), dtype=jnp.float32), 'clip_x': jnp.full((1,), 4.0, dtype=jnp.float32), 'clip_down': jnp.full((1,), 4.0, dtype=jnp.float32), 'w_gate': jax.random.normal(k2, (I, H), dtype=jnp.float32) * 0.02, 'w_up': jax.random.normal(k3, (I, H), dtype=jnp.float32) * 0.02, 'w_down': jax.random.normal(k4, (H, I), dtype=jnp.float32) * 0.02}
    _L0_ffn_all = _L0_ffn_setup()
    _L0_ffn_in = {k: v for k, v in _L0_ffn_all.items() if k in ('clip_x', 'clip_down', 'w_gate', 'w_up', 'w_down')}
    del _L0_ffn_all
    return {'x': x, 'src': src, 'dst': dst, 'L0_gnn_W': _L0_gnn_in['W'], 'L0_gnn_b': _L0_gnn_in['b'], 'L0_mix_Wq': _L0_mix_in['Wq'], 'L0_mix_bq': _L0_mix_in['bq'], 'L0_mix_Wk': _L0_mix_in['Wk'], 'L0_mix_bk': _L0_mix_in['bk'], 'L0_mix_Wv': _L0_mix_in['Wv'], 'L0_mix_bv': _L0_mix_in['bv'], 'L0_mix_Wo': _L0_mix_in['Wo'], 'L0_mix_bo': _L0_mix_in['bo'], 'L0_ffn_clip_x': _L0_ffn_in['clip_x'], 'L0_ffn_clip_down': _L0_ffn_in['clip_down'], 'L0_ffn_w_gate': _L0_ffn_in['w_gate'], 'L0_ffn_w_up': _L0_ffn_in['w_up'], 'L0_ffn_w_down': _L0_ffn_in['w_down']}

def reference(x, src, dst, L0_gnn_W, L0_gnn_b, L0_mix_Wq, L0_mix_bq, L0_mix_Wk, L0_mix_bk, L0_mix_Wv, L0_mix_bv, L0_mix_Wo, L0_mix_bo, L0_ffn_clip_x, L0_ffn_clip_down, L0_ffn_w_gate, L0_ffn_w_up, L0_ffn_w_down):
    import jax
    import jax.numpy as jnp

    def _L0_gnn_ref(x, edge_index, W, b):
        import jax, jax.numpy as jnp
        import numpy as np
        N_NODES = 1250
        N_EDGES = 20000
        DIM = 1024
        'GCNConv (add_self_loops=True, symmetric norm) -> Dropout(eval=identity) -> ReLU.'
        n = x.shape[0]
        loops = jnp.arange(n, dtype=edge_index.dtype)
        src = jnp.concatenate([edge_index[0], loops])
        dst = jnp.concatenate([edge_index[1], loops])
        deg = jax.ops.segment_sum(jnp.ones_like(dst, dtype=x.dtype), dst, num_segments=n)
        dinv = jnp.where(deg > 0, jax.lax.rsqrt(deg), jnp.zeros_like(deg))
        norm = dinv[src] * dinv[dst]
        h = x @ W
        msg = h[src] * norm[:, None]
        out = jax.ops.segment_sum(msg, dst, num_segments=n) + b
        return jax.nn.relu(out)

    def _L0_mix_ref(x, Wq, bq, Wk, bk, Wv, bv, Wo, bo):
        import jax, jax.numpy as jnp
        import numpy as np
        B, L, D = (2, 256, 1024)
        H = 16
        DH = D // H
        b, l, _ = x.shape

        def split_heads(t):
            return t.reshape(b, l, H, DH).transpose((0, 2, 1, 3))
        q = jax.nn.relu(split_heads(x @ Wq + bq))
        k = jax.nn.relu(split_heads(x @ Wk + bk))
        v = split_heads(x @ Wv + bv)
        context = jnp.einsum('bhld,bhkd->bhlk', q, k) / (l * DH)
        attn = jnp.einsum('bhlk,bhkd->bhld', context, v)
        attn = attn.transpose((0, 2, 1, 3)).reshape(b, l, D)
        return attn @ Wo + bo

    def _L0_ffn_ref(x, clip_x, clip_down, w_gate, w_up, w_down):
        import jax, jax.numpy as jnp
        import numpy as np
        QMAX = 127.0

        def _ste_round(v):
            return v + jax.lax.stop_gradient(jnp.round(v) - v)

        def _act_fake_quant(x, clip_factor):
            scale = jax.nn.sigmoid(clip_factor) * jnp.max(jnp.abs(x)) / QMAX
            return jnp.clip(_ste_round(x / scale), -QMAX - 1.0, QMAX) * scale

        def _weight_fake_quant(w):
            scale = jnp.max(jnp.abs(w), axis=1, keepdims=True) / QMAX
            return jnp.clip(_ste_round(w / scale), -QMAX - 1.0, QMAX) * scale
        xq = _act_fake_quant(x, clip_x[0])
        gate = jnp.einsum('bsh,ih->bsi', xq, _weight_fake_quant(w_gate))
        up = jnp.einsum('bsh,ih->bsi', xq, _weight_fake_quant(w_up))
        h = _act_fake_quant(jax.nn.silu(gate) * up, clip_down[0])
        return jnp.einsum('bsi,hi->bsh', h, _weight_fake_quant(w_down))
    edge_index = jnp.stack([src, dst])
    xn = _layernorm(x, axis=-1)
    x = x + _L0_gnn_ref(xn, edge_index, L0_gnn_W, L0_gnn_b) + _L0_mix_ref(xn[None], L0_mix_Wq, L0_mix_bq, L0_mix_Wk, L0_mix_bk, L0_mix_Wv, L0_mix_bv, L0_mix_Wo, L0_mix_bo)[0]
    x = x + _L0_ffn_ref(_layernorm(x, axis=-1)[None], L0_ffn_clip_x, L0_ffn_clip_down, L0_ffn_w_gate, L0_ffn_w_up, L0_ffn_w_down)[0]
    return x

_drawn_inputs = setup_inputs


def setup_inputs(seed=0):
    import zlib

    import numpy as np

    out = dict(_drawn_inputs(seed))
    spreads = {'L0_gnn_b': (0.0, 0.8),
     'L0_mix_bq': (0.0, 2.0),
     'L0_mix_bk': (0.0, 2.0),
     'L0_mix_bv': (0.0, 0.386),
     'L0_mix_bo': (0.0, 0.8)}
    factors = {'L0_mix_Wq': 7.568,
     'L0_mix_Wk': 8.0,
     'L0_mix_Wv': 6.493,
     'L0_mix_Wo': 2.804,
     'L0_gnn_W': 5.446,
     'L0_ffn_w_gate': 8.0,
     'L0_ffn_w_up': 8.0,
     'L0_ffn_w_down': 8.0}
    for name, (base, spread) in spreads.items():
        noise = np.random.default_rng([zlib.crc32(name.encode()), seed]).standard_normal(out[name].shape)
        drawn = base * np.exp(spread * noise) if base else spread * noise
        out[name] = jnp.asarray(drawn.astype(out[name].dtype))
    for name, factor in factors.items():
        out[name] = (out[name] * factor).astype(out[name].dtype)
    return out
```

```python
from contextlib import ExitStack

import concourse.bass as bass
from concourse import mybir

ALU = mybir.AluOpType
ACT = mybir.ActivationFunctionType
AX = mybir.AxisListType
F32 = mybir.dt.float32
BF16 = mybir.dt.bfloat16
I32 = mybir.dt.int32
U32 = mybir.dt.uint32
U16 = mybir.dt.uint16

P = 128
HALF = 512
N, D = 1250, 1024
T = -(-N // P)
LAST = N - (T - 1) * P
NP = T * P
K = D // P
HEADS, DH = 16, 64
PAIRS = HEADS // 2
E = 40000
EC = 125
C = E // EC
W = 16
WC = W * T
UNITS = 8
CT = C // T
PT = CT // 2
FF = 352
FB = -(-FF // P)
FR = [min(P, FF - P * b) for b in range(FB)]
QMAX = 127.0
MAGIC = 1.5 * 2.0 ** 23
EPS = 1e-5
EB = [(0, P), (P, P), (2 * P, C - 2 * P)]
NCH = [(0, 512), (512, 512), (1024, 256)]
assert E == EC * C and C == CT * T and CT == 4 * UNITS


def gps_layer(nc, x, src, dst, gnn_W, gnn_b, Wq, bq, Wk, bk, Wv, bv, Wo, bo,
              clip_x, clip_down, w_gate, w_up, w_down, out):
    with ExitStack() as ctx:
        def sb(name, shape, dt):
            return ctx.enter_context(nc.sbuf_tensor(name, shape, dt))

        def sem(name):
            return ctx.enter_context(nc.semaphore(name))

        bank = [ctx.enter_context(nc.psum_tensor(f"bank{i}", [P, HALF], F32)) for i in range(8)]
        proj, kv_acc, tp, adj_ps = bank[0:2], bank[2:4], bank[4:6], bank[6:8]

        qT_d = nc.dram_tensor("qT_d", [T, P, D], F32, kind="Internal").ap()
        g_d = nc.dram_tensor("g_d", [T, P, D], F32, kind="Internal").ap()
        x2_d = nc.dram_tensor("x2_d", [T, P, D], F32, kind="Internal").ap()

        big = sb("big", [P, 4 * K * D], F32)
        small = sb("small", [P, 11 * D], F32)

        def view(area, start, blocks, width):
            return area[:, start:start + blocks * width].rearrange("p (b w) -> p b w", w=width)

        wk, wv, wq, wg = [view(big, i * K * D, K, D) for i in range(4)]
        wo, mixW = wk, wv
        h_sb = view(big, 2 * K * D, T, D)
        free_b = 2 * K * D + T * D
        qT_t = [view(big, i * D, K, P) for i in range(2)]
        a_t = [view(big, 2 * D + i * T * P, T, P) for i in range(2)]
        x_t = [big[:, 2 * D + 2 * T * P + i * D:2 * D + 2 * T * P + (i + 1) * D] for i in range(2)]
        bo_b = big[:, free_b:free_b + D]
        gb_b = big[:, free_b + D:free_b + 2 * D]
        tmp_b = big[:, free_b + 2 * D:free_b + 3 * D]
        x2_t = [big[:, free_b + (3 + i) * D:free_b + (4 + i) * D] for i in range(2)]

        x_in = small[:, 0:D]
        xT = [view(small, (1 + i) * D, K, P) for i in range(2)]
        k_t, v_t, q_t, qT_o, g_o = [small[:, (3 + i) * D:(4 + i) * D] for i in range(5)]
        bk_b, bv_b, bq_b = [small[:, (8 + i) * D:(9 + i) * D] for i in range(3)]
        xn2 = view(small, 0, T, D)

        counts = sb("counts", [P, NP * T], U16)
        keyT = sb("keyT", [P, C], F32)
        loT = sb("loT", [P, C], F32)
        src_col = sb("src_col", [P, 2, 4], F32)
        span_max = sb("span_max", [1, 1], I32)
        base_row = sb("base_row", [1, C], I32)
        iota_w = sb("iota_w", [P, WC], BF16)
        iota_p = sb("iota_p", [P, P], BF16)
        hot_dst = sb("hot_dst", [P, 2, 2, WC], BF16)
        hot_src = sb("hot_src", [P, 2, 4, P], BF16)
        ident = sb("ident", [P, P], F32)
        half_neg = sb("half_neg", [P, T], F32)
        fin = sb("fin", [P, 48], F32)
        ones_r = sb("ones_r", [1, P], F32)
        stats = sb("stats", [P, 2, 6], F32)
        mv = sb("mv", [P, 2], F32)
        var_eps = sb("var_eps", [P, 1], F32)
        exponent = sb("exponent", [P, 1], F32)
        rstd = sb("rstd", [P, 1], F32)
        cols = sb("cols", [P, 64], F32)
        dinv = cols[:, 0:T]
        mx = cols[:, T:2 * T]
        ones = cols[:, 2 * T:2 * T + 1]
        neg_magic = cols[:, 21:22]

        e_src, e_dst, e_hi, e_lo = [view(small, (3 + i) * D, 3, P).bitcast(I32) for i in range(4)]
        e_key = view(small, 7 * D, 3, P)
        e_lof = view(small, 7 * D + 3 * P, 3, P)
        e_min = small[:, 6 * D + 512:6 * D + 512 + 4]
        e_span = small[:, 6 * D + 520:6 * D + 524]

        S = {n: sem(n) for n in (
            "consts", "pool_step", "edges_in", "bias_in", "wk_in0", "wv_in0", "wq_in0", "wg_in0", "wk_in1", "wv_in1", "wq_in1", "wg_in1", "x_in", "dve_step", "ln_step", "var_ready", "rstd_ready",
            "prep_tp", "prep_ev", "ln_done", "tp_full", "fill_moved", "unit_full", "dve_evac",
            "act_evac", "k_relu", "q_relu", "kv_done", "qT_stored", "g_stored", "hot_dst_ready",
            "src_col_ready", "hot_src_ready", "adj_mm", "adj_added")}

        with nc.Block() as block:

            @block.sync
            def _(sp):
                for e, a in ((e_dst, dst), (e_src, src)):
                    ev = a.rearrange("(c e) -> c e", e=EC)
                    sp.dma_start(e[:, 0:2, 0:EC], ev[0:2 * P].rearrange("(b p) e -> p b e", p=P)).then_inc(S["edges_in"], 16)
                    sp.dma_start(e[0:EB[2][1], 2, 0:EC], ev[2 * P:C]).then_inc(S["edges_in"], 16)
                sp.dma_start(x_in, x[0:P, :]).then_inc(S["x_in"], 16)
                for w_sb, w, s in ((wk, Wk, "wk_in"), (wv, Wv, "wv_in"), (wq, Wq, "wq_in"), (wg, gnn_W, "wg_in")):
                    wd = w.rearrange("(k p) n -> p k n", p=P)
                    for h in range(2):
                        sp.dma_start(w_sb[:, :, h * HALF:(h + 1) * HALF], wd[:, :, h * HALF:(h + 1) * HALF]).then_inc(S[f"{s}{h}"], 16)
                sp.wait_ge(S["prep_ev"], 1)
                for b_sb, b in ((bk_b, bk), (bv_b, bv), (bq_b, bq)):
                    sp.dma_start(b_sb, b.rearrange("(a n) -> a n", a=1).broadcast_to([P, D])).then_inc(S["bias_in"], 16)
                sp.wait_ge(S["tp_full"], 2)
                sp.dma_start(x_in, x[P:2 * P, :]).then_inc(S["x_in"], 16)

                def store(t, last_tile=False):
                    sp.wait_ge(S["act_evac"], 2 * t + 2)
                    sp.dma_start(g_d[bass.ds(t, 1)].rearrange("a p d -> (a p) d"), g_o).then_inc(S["g_stored"], 16)
                    sp.wait_ge(S["fill_moved"], 40 if last_tile else 4 * t + 6)
                    sp.dma_start(qT_d[bass.ds(t, 1)].rearrange("a p d -> (a p) d"), qT_o).then_inc(S["qT_stored"], 16)

                with sp.Fori(0, T - 3) as t:
                    sp.wait_ge(S["tp_full"], 4 * t + 4)
                    sp.dma_start(x_in, x[bass.ds((t + 2) * P, P), :]).then_inc(S["x_in"], 16)
                    store(t)
                sp.wait_ge(S["tp_full"], 4 * (T - 3) + 4)
                sp.dma_start(x_in[0:LAST, :], x[(T - 1) * P:N, :]).then_inc(S["x_in"], 16)
                for t in range(T - 3, T):
                    store(t, t == T - 1)
                sp.wait_ge(S["g_stored"], 16 * T)
                sp.wait_ge(S["qT_stored"], 16 * T)

            @block.gpsimd
            def _(pool):
                pool.memset(ident[:, :], 0.0).then_inc(S["pool_step"], 1)
                pool.memset(exponent[:, :], -0.5).then_inc(S["pool_step"], 1)
                pool.iota(iota_w[:, :], [[1, WC]], base=0, channel_multiplier=0,
                          allow_small_or_imprecise_dtypes=True).then_inc(S["consts"], 1)
                pool.iota(iota_p[:, :], [[1, P]], base=0, channel_multiplier=0,
                          allow_small_or_imprecise_dtypes=True).then_inc(S["consts"], 1)
                pool.wait_ge(S["pool_step"], 2)
                pool.affine_select(out=ident[:, :], in_=ident[:, :], compare_op=ALU.not_equal, fill=1.0, base=0,
                                   pattern=[[-1, P]], channel_multiplier=1).then_inc(S["consts"], 1)

                def one_hot_sources(g, par):
                    c = 4 * g
                    pool.tensor_copy(src_col[0:EC, par, :], loT[0:EC, bass.ds(c, 4)]).then_inc(S["src_col_ready"], 1)
                    pool.drain()
                    for i in range(4):
                        pool.tensor_scalar(hot_src[0:EC, par, i, :], iota_p[0:EC, :], src_col[0:EC, par, i:i + 1], None,
                                           ALU.is_equal).then_inc(S["hot_src_ready"], 1)

                def inverse_deviation(n):
                    pool.wait_ge(S["var_ready"], n + 1)
                    pool.tensor_tensor(rstd[:, :], var_eps[:, :], exponent[:, :], ALU.pow).then_inc(S["rstd_ready"], 1)

                inverse_deviation(0)
                pool.wait_ge(S["prep_ev"], 2)

                def tile(t, first, last_tile):
                    for j in range(UNITS):
                        g = UNITS * t + j
                        if not (first and j < 2):
                            pool.wait_ge(S["adj_mm"], 2 * g - 2)
                        one_hot_sources(g, j % 2)
                        if j == 3 and not last_tile:
                            inverse_deviation(t + 1)

                tile(0, True, False)
                with pool.Fori(1, T - 1) as t:
                    tile(t, False, False)
                tile(T - 1, False, True)

            @block.tensor
            def _(pe):
                pe.wait_ge(S["consts"], 3)
                pe.wait_ge(S["prep_tp"], 1)
                for b, (c0, n) in enumerate(EB):
                    pe.transpose(bank[0][0:EC, c0:c0 + n], e_key[0:n, b, 0:EC], ident[0:n, 0:n])
                    pe.transpose(bank[1][0:EC, c0:c0 + n], e_lof[0:n, b, 0:EC], ident[0:n, 0:n])
                    pe.transpose(bank[3][0:1, c0:c0 + n], e_span[0:n, b:b + 1], ident[0:n, 0:n])
                    last = pe.transpose(bank[2][0:1, c0:c0 + n], e_min[0:n, b:b + 1], ident[0:n, 0:n])
                last.then_inc(S["unit_full"], 1)

                def transposes(source, f, wait_reader):
                    for j in range(2):
                        if wait_reader:
                            pe.wait_ge(S["fill_moved"], f + j - 1)
                        for k in range(4):
                            last = pe.transpose(tp[j][:, k * P:(k + 1) * P],
                                                source[:, (4 * j + k) * P:(4 * j + k + 1) * P], ident[:, :])
                        last.then_inc(S["tp_full"], 1)

                def adj_pair(q, i, g, gp, first):
                    pe.wait_ge(S["hot_src_ready"], 4 * g + 4)
                    pe.wait_ge(S["hot_dst_ready"], 2 * q + 2)
                    if not first:
                        pe.wait_ge(S["adj_added"], 2 * q - 2)
                    for cc in range(2):
                        last = pe.matmul(adj_ps[i][:, cc * WC:(cc + 1) * WC], hot_src[0:EC, gp, 2 * i + cc, :],
                                         hot_dst[0:EC, i, cc, :], start=(cc == 0), stop=True, skip_group_check=True)
                    last.then_inc(S["adj_mm"], 1)

                pe.wait_ge(S["ln_done"], 1)
                transposes(x_in, 0, False)

                def tile(t, par, rows, first, last_tile):
                    units = [(wk, "wk_in"), (wv, "wv_in"), (wq, "wq_in"), (wg, "wg_in")]
                    for j in range(UNITS):
                        w, arrived = units[j // 2]
                        half = j % 2
                        if first:
                            pe.wait_ge(S[f"{arrived}{half}"], 16)
                        if j == 0:
                            pe.wait_ge(S["fill_moved"], 2 if first else 4 * t)
                        if j < 2:
                            if not first:
                                pe.wait_ge(S["act_evac"], 2 * t - 1 + j)
                            else:
                                pe.wait_ge(S["prep_ev"], 3)
                        else:
                            pe.wait_ge(S["dve_evac"], 6 * t + j - 1)
                        for k in range(K):
                            last = pe.matmul(proj[half][:, :], xT[par][:, k, :], w[:, k, half * HALF:(half + 1) * HALF],
                                             start=(k == 0), stop=(k == K - 1))
                            if k == K - 1:
                                last.then_inc(S["unit_full"], 1)
                            if k % 4 == 3:
                                i = k // 4
                                adj_pair(PT * t + 2 * j + i, i, UNITS * t + j, j % 2, first and j == 0)
                        if j == 3 and not last_tile:
                            pe.wait_ge(S["ln_done"], t + 2)
                            transposes(x_in, 4 * t + 2, True)
                        if j == 4:
                            pe.wait_ge(S["k_relu"], 2 * t + 2)
                            pe.wait_ge(S["dve_evac"], 6 * t + 4)
                            for p in range(PAIRS):
                                o = kv_acc[p // 4][:, (p % 4) * P:(p % 4 + 1) * P]
                                last = pe.matmul(o, v_t[0:rows, p * P:(p + 1) * P], k_t[0:rows, p * P:(p + 1) * P],
                                                 start=(first and p % 4 == 0), stop=last_tile, skip_group_check=True)
                            last.then_inc(S["kv_done"], 1)
                    pe.wait_ge(S["q_relu"], 2 * t + 2)
                    transposes(q_t, 4 * t + (2 if last_tile else 4), True)

                tile(0, 0, P, True, False)
                with pe.Fori(0, (T - 2) // 2) as t2:
                    t = 2 * t2 + 1
                    tile(t, 1, P, False, False)
                    tile(t + 1, 0, P, False, False)
                tile(T - 1, (T - 1) % 2, LAST, False, True)

            @block.scalar
            def _(act):
                def fill(f, j, dst):
                    act.wait_ge(S["tp_full"], f + j + 1)
                    act.activation(dst, tp[j][:, :], ACT.Copy).then_inc(S["fill_moved"], 1)

                def xT_fill(f, par):
                    flat = xT[par].rearrange("p k n -> p (k n)")
                    for j in range(2):
                        fill(f, j, flat[:, j * HALF:(j + 1) * HALF])

                xT_fill(0, 0)

                def tile(t, par, first, last_tile):
                    for h in range(2):
                        act.wait_ge(S["dve_evac"], 6 * t + 1 + h)
                        kh = k_t[:, h * HALF:(h + 1) * HALF]
                        act.activation(kh, kh, ACT.Relu).then_inc(S["k_relu"], 1)
                    if not last_tile:
                        xT_fill(4 * t + 2, 1 - par)
                    for h in range(2):
                        act.wait_ge(S["dve_evac"], 6 * t + 5 + h)
                        qh = q_t[:, h * HALF:(h + 1) * HALF]
                        act.activation(qh, qh, ACT.Relu).then_inc(S["q_relu"], 1)
                    for h in range(2):
                        act.wait_ge(S["unit_full"], UNITS * t + 8 + h)
                        if h == 0 and not first:
                            act.wait_ge(S["g_stored"], 16 * t)
                        act.activation(g_o[:, h * HALF:(h + 1) * HALF], proj[h][:, :], ACT.Copy).then_inc(S["act_evac"], 1)
                    if not first:
                        act.wait_ge(S["qT_stored"], 16 * t)
                    f = 4 * t + (2 if last_tile else 4)
                    for j in range(2):
                        fill(f, j, qT_o[:, j * HALF:(j + 1) * HALF])

                tile(0, 0, True, False)
                with act.Fori(0, (T - 2) // 2) as t2:
                    t = 2 * t2 + 1
                    tile(t, 1, False, False)
                    tile(t + 1, 0, False, False)
                tile(T - 1, (T - 1) % 2, False, True)

            @block.vector
            def _(dve):
                steps = [0]

                def step(ins):
                    steps[0] += 1
                    ins.then_inc(S["dve_step"], 1)
                    dve.wait_ge(S["dve_step"], steps[0])

                step(dve.memset(counts[:, :].bitcast(U32), 0))
                step(dve.memset(cols[:, :], 0.0))
                dve.wait_ge(S["edges_in"], 64)
                for b, (_, n) in enumerate(EB):
                    step(dve.tensor_reduce(e_min[0:n, b:b + 1], e_dst[0:n, b, 0:EC], AX.X, ALU.min))
                    step(dve.tensor_reduce(e_span[0:n, b:b + 1], e_dst[0:n, b, 0:EC], AX.X, ALU.max))
                    step(dve.tensor_tensor(e_span[0:n, b:b + 1], e_span[0:n, b:b + 1], e_min[0:n, b:b + 1], ALU.subtract))
                    step(dve.tensor_scalar(e_hi[0:n, b, 0:EC], e_src[0:n, b, 0:EC], 7, None, ALU.logical_shift_right))
                    step(dve.tensor_scalar(e_lo[0:n, b, 0:EC], e_src[0:n, b, 0:EC], P - 1, None, ALU.bitwise_and))
                    step(dve.tensor_copy(e_lof[0:n, b, 0:EC], e_lo[0:n, b, 0:EC]))
                    step(dve.tensor_scalar(e_key[0:n, b, 0:EC], e_dst[0:n, b, 0:EC], e_min[0:n, b:b + 1], float(T),
                                           ALU.subtract, ALU.mult))
                    step(dve.tensor_tensor(e_key[0:n, b, 0:EC], e_key[0:n, b, 0:EC], e_hi[0:n, b, 0:EC], ALU.add))
                dve.nop().then_inc(S["prep_tp"], 1)
                dve.wait_ge(S["unit_full"], 1)
                step(dve.tensor_reduce(span_max[:, :], bank[3][0:1, 0:C], AX.X, ALU.max))
                dve.tensor_scalar(base_row[:, :], bank[2][0:1, 0:C], float(T), None, ALU.mult).then_inc(S["prep_ev"], 1)
                dve.tensor_copy(loT[0:EC, :], bank[1][0:EC, 0:C]).then_inc(S["prep_ev"], 1)
                dve.tensor_copy(keyT[0:EC, :], bank[0][0:EC, 0:C]).then_inc(S["prep_ev"], 1)
                dve.wait_ge(S["consts"], 3)
                cv = counts[:, :].rearrange("p (n s) -> p n s", s=T)
                for t in range(T):
                    r = P if t < T - 1 else LAST
                    step(dve.tensor_copy(cv[:, t * P:t * P + r, t], ident[:, 0:r]))
                dve.wait_ge(S["prep_ev"], 3)

                def one_hot_dst(q, i):
                    for cc in range(2):
                        dve.tensor_scalar(hot_dst[0:EC, i, cc, :], iota_w[0:EC, :], keyT[0:EC, bass.ds(2 * q + cc, 1)],
                                          None, ALU.is_equal).then_inc(S["hot_dst_ready"], 1)

                def adj_add(q, i, first):
                    dve.wait_ge(S["adj_mm"], q + 1)
                    for cc in range(2):
                        c = 2 * q + cc
                        at = dve.value_load(base_row[0:1, bass.ds(c, 1)], min_val=0, max_val=(N - 1) * T)
                        if not (first and cc == 0):
                            dve.wait_ge(S["adj_added"], c)
                        window = counts[:, bass.ds(at, WC)]
                        dve.tensor_tensor(window, adj_ps[i][:, cc * WC:(cc + 1) * WC], window,
                                          ALU.add).then_inc(S["adj_added"], 1)

                ln_step = [0]

                def layernorm(t, count):
                    for h in range(2):
                        dve.bn_stats(stats[:, h, :], x_in[:, h * HALF:(h + 1) * HALF]).then_inc(S["ln_step"], 1)
                    dve.drain()
                    dve.bn_aggr(mv[:, :], stats[:, :, :].rearrange("p a b -> p (a b)")).then_inc(S["ln_step"], 1)
                    dve.wait_ge(S["ln_step"], 3 * count + 3)
                    dve.tensor_scalar(var_eps[:, :], mv[:, 1:2], EPS, None, ALU.add).then_inc(S["var_ready"], 1)
                    dve.wait_ge(S["rstd_ready"], count + 1)
                    dve.tensor_scalar(x_in[:, :], x_in[:, :], mv[:, 0:1], rstd[:, 0:1], ALU.subtract,
                                      ALU.mult).then_inc(S["ln_done"], 1)

                dve.wait_ge(S["x_in"], 16)
                layernorm(0, 0)
                for i in range(2):
                    one_hot_dst(i, i)

                def tile(t, first, last_tile):
                    for j in range(UNITS):
                        for i in range(2):
                            q = PT * t + 2 * j + i
                            adj_add(q, i, first and j == 0 and i == 0)
                            if not (last_tile and j == UNITS - 1):
                                one_hot_dst(q + 2, i)
                        half = j % 2
                        if j < 6:
                            o = (k_t, v_t, q_t)[j // 2]
                            b = (bk_b, bv_b, bq_b)[j // 2]
                            if first and j == 0:
                                dve.wait_ge(S["bias_in"], 48)
                            if not first and j in (0, 2):
                                dve.wait_ge(S["kv_done"], t)
                            if not first and j == 4:
                                dve.wait_ge(S["tp_full"], 4 * t + 2)
                            dve.wait_ge(S["unit_full"], UNITS * t + j + 2)
                            s = slice(half * HALF, (half + 1) * HALF)
                            dve.tensor_tensor(o[:, s], proj[half][:, :], b[:, s], ALU.add).then_inc(S["dve_evac"], 1)
                        if j == 1 and not last_tile:
                            dve.wait_ge(S["x_in"], 16 * t + 32)
                            layernorm(t + 1, t + 1)

                tile(0, True, False)
                with dve.Fori(0, (T - 2) // 2) as t2:
                    t = 2 * t2 + 1
                    tile(t, False, False)
                    tile(t + 1, False, False)
                tile(T - 1, False, True)


        SE = {n: sem("e_" + n) for n in ("moved_on", "hot", "mm", "added")}
        with nc.Block() as block:
            WINDOWS = -(-N // W)

            @block.tensor
            def _(pe):
                span = pe.value_load(span_max[0:1, 0:1], min_val=0, max_val=N)
                with pe.If(span >= W):
                    with pe.Fori(1, WINDOWS) as k:
                        with pe.Fori(0, C) as c:
                            pe.wait_ge(SE["hot"], 2 * ((k - 1) * C + c) + 2)
                            pe.matmul(adj_ps[0][:, 0:WC], hot_src[0:EC, 0, 0, :], hot_dst[0:EC, 0, 0, :], start=True,
                                      stop=True).then_inc(SE["mm"], 1)

            @block.vector
            def _(dve):
                span = dve.value_load(span_max[0:1, 0:1], min_val=0, max_val=N)
                with dve.If(span >= W):
                    with dve.Fori(1, WINDOWS) as k:
                        dve.tensor_scalar(keyT[0:EC, :], keyT[0:EC, :], float(-WC), None, ALU.add).then_inc(SE["moved_on"], 1)
                        dve.tensor_scalar(base_row[:, :], base_row[:, :], float(WC), float(N * T), ALU.add,
                                          ALU.min).then_inc(SE["moved_on"], 1)
                        dve.drain()
                        with dve.Fori(0, C) as c:
                            dve.tensor_scalar(hot_dst[0:EC, 0, 0, :], iota_w[0:EC, :], keyT[0:EC, bass.ds(c, 1)],
                                              None, ALU.is_equal).then_inc(SE["hot"], 1)
                            dve.tensor_scalar(hot_src[0:EC, 0, 0, :], iota_p[0:EC, :], loT[0:EC, bass.ds(c, 1)],
                                              None, ALU.is_equal).then_inc(SE["hot"], 1)
                            at = dve.value_load(base_row[0:1, bass.ds(c, 1)], min_val=0, max_val=N * T)
                            window = counts[:, bass.ds(at, WC)]
                            dve.wait_ge(SE["mm"], (k - 1) * C + c + 1)
                            dve.tensor_tensor(window, adj_ps[0][:, 0:WC], window, ALU.add).then_inc(SE["added"], 1)
                            dve.wait_ge(SE["added"], (k - 1) * C + c + 1)


        SM = {n: sem("m_" + n) for n in (
            "wo_in", "h_in", "bias_in", "kvs_zero", "kvs", "sources", "deg_full", "deg_ready", "dinv", "prod_full",
            "prod_moved", "h_scaled")}
        kvs = view(small, 10 * D, PAIRS, P)
        sources = small[:, 0:NP]
        with nc.Block() as block:
            @block.sync
            def _(sp):
                wod = Wo.rearrange("(k p) n -> p k n", p=P)
                sp.dma_start(wo, wod).then_inc(SM["wo_in"], 16)
                sp.dma_start(h_sb, g_d.rearrange("t p d -> p t d")).then_inc(SM["h_in"], 16)
                for b_sb, b in ((bo_b, bo), (gb_b, gnn_b)):
                    sp.dma_start(b_sb, b.rearrange("(a n) -> a n", a=1).broadcast_to([P, D])).then_inc(SM["bias_in"], 16)
                sp.wait_ge(SM["bias_in"], 32)

            @block.gpsimd
            def _(pool):
                pool.memset(half_neg[:, :], -0.5).then_inc(SM["deg_ready"], 1)
                pool.wait_ge(SM["deg_ready"], 2)
                pool.tensor_tensor(dinv, dinv, half_neg[:, :], ALU.pow).then_inc(SM["dinv"], 1)

            @block.vector
            def _(dve):
                dve.memset(kvs, 0.0).then_inc(SM["kvs_zero"], 1)
                dve.memset(ones, 1.0).then_inc(SM["kvs_zero"], 1)
                dve.wait_ge(SM["kvs_zero"], 2)
                for b in range(2):
                    acc = kv_acc[b][:, :].rearrange("p (q n) -> p q n", n=P)
                    for h in range(2):
                        r = slice(h * DH, (h + 1) * DH)
                        dve.tensor_scalar(kvs[r, 4 * b:4 * b + 4, r], acc[r, :, r], 1.0 / (N * DH), None,
                                          ALU.mult).then_inc(SM["kvs"], 1)
                dve.tensor_reduce(sources, counts[:, :].rearrange("p (n s) -> p n s", s=T), AX.X,
                                  ALU.add).then_inc(SM["sources"], 1)
                dve.wait_ge(SM["deg_full"], 1)
                dve.tensor_scalar(dinv, bank[4][:, 0:T], 1.0, None, ALU.max).then_inc(SM["deg_ready"], 1)
                dve.wait_ge(SM["dinv"], 1)
                dve.wait_ge(SM["h_in"], 16)
                for t in range(T):
                    dve.tensor_scalar(h_sb[:, t, :], h_sb[:, t, :], dinv[:, t:t + 1], None,
                                      ALU.mult).then_inc(SM["h_scaled"], 1)

            @block.tensor
            def _(pe):
                pe.wait_ge(SM["kvs"], 4)
                pe.wait_ge(SM["wo_in"], 16)
                for i in range(2 * PAIRS):
                    p, n = i // 2, i % 2
                    if i >= 2:
                        pe.wait_ge(SM["prod_moved"], i - 1)
                    pe.matmul(proj[n][:, :], kvs[:, p, :], wo[:, p, n * HALF:(n + 1) * HALF], start=True,
                              stop=True).then_inc(SM["prod_full"], 1)
                pe.wait_ge(SM["sources"], 1)
                for t in range(T):
                    last = pe.matmul(bank[4][:, t:t + 1], sources[:, t * P:(t + 1) * P], ones, start=True, stop=True,
                                     skip_group_check=True)
                last.then_inc(SM["deg_full"], 1)

            @block.scalar
            def _(act):
                for i in range(2 * PAIRS):
                    p, n = i // 2, i % 2
                    act.wait_ge(SM["prod_full"], i + 1)
                    act.activation(mixW[:, p, n * HALF:(n + 1) * HALF], proj[n][:, :], ACT.Copy).then_inc(SM["prod_moved"], 1)


        SB = {n: sem("b_" + n) for n in (
            "qT_in0", "qT_in1", "x_in0", "x_in1", "x_bias", "a_ready", "mix_full", "agg_full", "mix_moved", "agg_moved",
            "step", "x2_ready", "x2_st0", "x2_st1", "var", "rstd", "ln_done", "mx")}
        with nc.Block() as block:
            @block.sync
            def _(sp):
                def load(t, par, first, rows):
                    if not first:
                        sp.wait_ge(SB["mix_full"], 2 * t - 2)
                    sp.dma_start(qT_t[par], qT_d[bass.ds(t, 1)].rearrange("a p (k n) -> p (a k) n", n=P)).then_inc(SB[f"qT_in{par}"], 16)
                    if not first:
                        sp.wait_ge(SB["mix_moved"], 2 * t - 2)
                    sp.dma_start(x_t[par][0:rows, :], x[bass.ds(P * t, rows), :]).then_inc(SB[f"x_in{par}"], 16)

                def store(t, par):
                    sp.wait_ge(SB["x2_ready"], t + 1)
                    sp.dma_start(x2_d[bass.ds(t, 1)].rearrange("a p d -> (a p) d"), x2_t[par]).then_inc(SB[f"x2_st{par}"], 16)

                load(0, 0, True, P)
                load(1, 1, True, P)
                with sp.Fori(0, (T - 4) // 2 + 0) as t2:
                    for par in range(2):
                        store(2 * t2 + par, par)
                        load(2 * t2 + par + 2, par, False, P)
                store(T - 4, 0)
                load(T - 2, 0, False, P)
                store(T - 3, 1)
                load(T - 1, 1, False, LAST)
                store(T - 2, 0)
                store(T - 1, 1)
                sp.wait_ge(SB["x2_st0"], 16 * (T // 2))
                sp.wait_ge(SB["x2_st1"], 16 * (T // 2))

            def over_tiles(eng, tile):
                tile(0, 0, 0, True, False)
                tile(1, 1, 0, True, False)
                with eng.Fori(1, T // 2 - 1) as t2:
                    for par in range(2):
                        tile(2 * t2 + par, par, t2, False, False)
                tile(T - 2, 0, T // 2 - 1, False, False)
                tile(T - 1, 1, T // 2 - 1, False, True)

            @block.gpsimd
            def _(pool):
                def tile(t, par, t2, first, last_tile):
                    pool.wait_ge(SB[f"x_in{par}"], 16 * t2 + 16)
                    pool.tensor_tensor(x_t[par], x_t[par], bo_b, ALU.add).then_inc(SB["x_bias"], 1)
                    pool.wait_ge(SB["var"], t + 1)
                    pool.tensor_tensor(rstd[:, :], var_eps[:, :], exponent[:, :], ALU.pow).then_inc(SB["rstd"], 1)

                over_tiles(pool, tile)

            @block.scalar
            def _(act):
                def tile(t, par, t2, first, last_tile):
                    if not first:
                        act.wait_ge(SB["agg_full"], 2 * t - 2)
                    act.activation(a_t[par], counts[:, bass.ds(t * P * T, P * T)].rearrange("p (n s) -> p s n", s=T),
                                   ACT.Copy).then_inc(SB["a_ready"], 1)

                over_tiles(act, tile)

            @block.tensor
            def _(pe):
                def tile(t, par, t2, first, last_tile):
                    for n in range(2):
                        if n == 0:
                            pe.wait_ge(SB[f"qT_in{par}"], 16 * t2 + 16)
                        if not (isinstance(t, int) and t == 0):
                            pe.wait_ge(SB["mix_moved"], 2 * t - 1 + n)
                        for k in range(K):
                            last = pe.matmul(proj[n][:, :], qT_t[par][:, k, :], mixW[:, k, n * HALF:(n + 1) * HALF],
                                             start=(k == 0), stop=(k == K - 1))
                        last.then_inc(SB["mix_full"], 1)
                    for n in range(2):
                        if n == 0:
                            pe.wait_ge(SB["a_ready"], t + 1)
                        if not (isinstance(t, int) and t == 0):
                            pe.wait_ge(SB["agg_moved"], 2 * t - 1 + n)
                        for s in range(T):
                            last = pe.matmul(adj_ps[n][:, :], a_t[par][:, s, :], h_sb[:, s, n * HALF:(n + 1) * HALF],
                                             start=(s == 0), stop=(s == T - 1))
                        last.then_inc(SB["agg_full"], 1)

                over_tiles(pe, tile)

            @block.vector
            def _(dve):
                def tile(t, par, t2, first, last_tile):
                    x2 = x2_t[par]
                    if not first:
                        dve.wait_ge(SB[f"x2_st{par}"], 16 * t2)
                    dve.wait_ge(SB["x_bias"], t + 1)
                    for n in range(2):
                        s = slice(n * HALF, (n + 1) * HALF)
                        dve.wait_ge(SB["mix_full"], 2 * t + n + 1)
                        dve.tensor_tensor(x2[:, s], proj[n][:, :], x_t[par][:, s], ALU.add).then_inc(SB["mix_moved"], 1)
                    for n in range(2):
                        s = slice(n * HALF, (n + 1) * HALF)
                        dve.wait_ge(SB["agg_full"], 2 * t + n + 1)
                        dve.scalar_tensor_tensor(tmp_b[:, s], adj_ps[n][:, :], dinv[:, bass.ds(t, 1)], gb_b[:, s],
                                                 ALU.mult, ALU.add).then_inc(SB["agg_moved"], 1)
                        dve.wait_ge(SB["agg_moved"], 2 * t + n + 1)
                        dve.wait_ge(SB["mix_moved"], 2 * t + n + 1)
                        dve.scalar_tensor_tensor(x2[:, s], tmp_b[:, s], 0.0, x2[:, s], ALU.max,
                                                 ALU.add).then_inc(SB["step"], 1)
                        dve.wait_ge(SB["step"], 5 * t + 2 * n + 1)
                        dve.bn_stats(stats[:, n, :], x2[:, s]).then_inc(SB["step"], 1)
                    dve.nop().then_inc(SB["x2_ready"], 1)
                    dve.drain()
                    dve.bn_aggr(mv[:, :], stats[:, :, :].rearrange("p a b -> p (a b)")).then_inc(SB["step"], 1)
                    dve.wait_ge(SB["step"], 5 * t + 5)
                    dve.tensor_scalar(var_eps[:, :], mv[:, 1:2], EPS, None, ALU.add).then_inc(SB["var"], 1)
                    dve.wait_ge(SB["rstd"], t + 1)
                    xn = xn2[:, bass.ds(t, 1), :].rearrange("p a d -> p (a d)")
                    dve.tensor_scalar(xn, x2, mv[:, 0:1], rstd[:, 0:1], ALU.subtract, ALU.mult).then_inc(SB["ln_done"], 1)
                    dve.wait_ge(SB["ln_done"], t + 1)
                    r = LAST if last_tile else P
                    dve.tensor_reduce(mx[0:r, bass.ds(t, 1)], xn2[0:r, bass.ds(t, 1), :].rearrange("p a d -> p (a d)"), AX.X, ALU.max,
                                      apply_absolute_value=True).then_inc(SB["mx"], 1)

                over_tiles(dve, tile)


        def region(start, blocks, width, dt=F32):
            words = blocks * width // (2 if dt == BF16 else 1)
            a = big[:, start:start + words]
            if dt == BF16:
                a = a.bitcast(BF16)
            return a.rearrange("p (b w) -> p b w", w=width), start + words

        raw_g, at = region(0, FB, D)
        raw_u, at = region(at, FB, D)
        raw_d, at = region(at, K, FF)
        wguT, at = region(at, K * 2, FF, BF16)
        wdT, at = region(at, FB, D, BF16)
        xqT, at = region(at, K, NP, BF16)
        hT, at = region(at, FB, NP)
        hq, at = region(at, FB, NP, BF16)
        d_row, at = region(at, 1, D)
        x2_c = [None, None]
        x2_c[0], at = region(at, 1, D)
        x2_c[1], at = region(at, 1, D)
        sg, _ = region(0, 2, HALF)
        q_t = [region(2 * D + i * D, 1, D)[0] for i in range(2)]
        q_t = [hT[:, 0:1, 0:D], hT[:, 1:2, 0:D]]
        ones_m = x2_c[0][:, 0, 0:P]
        diag, _ = region(at, K, P)
        assert at + D <= 4 * K * D
        neg_magic_c = cols[:, 21:22]
        s_x, rs_x, s_d, rs_d = [cols[:, 22 + i:23 + i] for i in range(4)]
        m_col = cols[:, 26:27]
        wsc = cols[:, 27:27 + 2 * FB + K]
        wrc = fin[:, 0:2 * FB + K]
        gus = fin[:, 16:16 + 2 * FB]
        mh = fin[:, 24:24 + 9]
        row = fin[0:1, 40:48]
        SC = {n: sem("c_" + n) for n in (
            "raw_in", "clip_in", "step", "m_T", "row", "s_row", "s_bc", "exp", "wq_ready", "wT_full", "wT_moved",
            "diag", "drow_full", "drow", "q1", "q_ready", "qT_full", "qT_moved", "gate_full", "gate_moved", "up_moved",
            "silu", "hmax", "h_rounded", "hq", "y_full", "y_moved", "x2_in0", "x2_in1", "y_ready", "out0", "out1", "m_ready")}
        blocks_w = [(m, b) for m in range(2) for b in range(FB)]

        with nc.Block() as block:
            @block.sync
            def _(sp):
                for raw, w in ((raw_g, w_gate), (raw_u, w_up)):
                    sp.dma_start(raw[:, 0:2, :], w[0:2 * P, :].rearrange("(b p) d -> p b d", p=P)).then_inc(SC["raw_in"], 16)
                    sp.dma_start(raw[0:FR[2], 2, :], w[2 * P:FF, :]).then_inc(SC["raw_in"], 16)
                sp.dma_start(raw_d, w_down.rearrange("(k p) i -> p k i", p=P)).then_inc(SC["raw_in"], 16)
                sp.dma_start(row[:, 0:1], clip_x.rearrange("(a n) -> a n", a=1)).then_inc(SC["clip_in"], 16)
                sp.dma_start(row[:, 1:2], clip_down.rearrange("(a n) -> a n", a=1)).then_inc(SC["clip_in"], 16)

                def load(t, par):
                    sp.dma_start(x2_c[par], x2_d[bass.ds(t, 1)].rearrange("a p d -> p a d")).then_inc(SC[f"x2_in{par}"], 16)

                def store(t, par, rows):
                    sp.wait_ge(SC["y_ready"], 2 * t + 2)
                    sp.dma_start(out[bass.ds(P * t, rows), :], x2_c[par][0:rows, 0, :]).then_inc(SC[f"out{par}"], 16)

                sp.wait_ge(SC["drow"], 2)
                load(0, 0)
                load(1, 1)
                with sp.Fori(0, T // 2 - 1) as t2:
                    for par in range(2):
                        store(2 * t2 + par, par, P)
                        sp.wait_ge(SC[f"out{par}"], 16 * t2 + 16)
                        load(2 * t2 + par + 2, par)
                store(T - 2, 0, P)
                store(T - 1, 1, LAST)
                sp.wait_ge(SC["out0"], 16 * (T // 2))
                sp.wait_ge(SC["out1"], 16 * (T // 2))

            @block.scalar
            def _(act):
                act.wait_ge(SC["clip_in"], 32)
                act.activation(row[:, 2:4], row[:, 0:2], ACT.Exp, scale=-1.0).then_inc(SC["exp"], 1)
                act.wait_ge(SC["m_ready"], 1)
                for i, (m, b) in enumerate(blocks_w):
                    for j in range(2):
                        f = 2 * i + j
                        n = FR[b]
                        act.wait_ge(SC["wT_full"], f + 1)
                        act.activation(wguT[:, :, :].rearrange("p (k m) f -> p k m f", m=2)[:, 4 * j:4 * j + 4, m, b * P:b * P + n],
                                       bank[4 + j][:, 0:4 * n].rearrange("p (k n) -> p k n", n=n), ACT.Identity,
                                       bias=neg_magic_c).then_inc(SC["wT_moved"], 1)
                for i, b in enumerate(range(FB)):
                    for j in range(2):
                        f = 2 * (len(blocks_w) + i) + j
                        n = FR[b]
                        act.wait_ge(SC["wT_full"], f + 1)
                        act.activation(wdT[0:n, b, j * HALF:(j + 1) * HALF], bank[4 + j][0:n, :], ACT.Identity,
                                       bias=neg_magic_c[0:n]).then_inc(SC["wT_moved"], 1)

                def xq_tile(t):
                    for j in range(2):
                        act.wait_ge(SC["qT_full"], 2 * t + j + 1)
                        act.activation(xqT[:, 4 * j:4 * j + 4, bass.ds(t * P, P)],
                                       bank[6 + j][:, :].rearrange("p (k n) -> p k n", n=P), ACT.Identity,
                                       bias=neg_magic_c).then_inc(SC["qT_moved"], 1)
                with act.Fori(0, T) as t:
                    xq_tile(t)
                u = 0
                for c, (c0, w) in enumerate(NCH):
                    for b in range(FB):
                        n = FR[b]
                        act.wait_ge(SC["gate_full"], 2 * u + 1)
                        if u >= 2:
                            act.wait_ge(SC["up_moved"], u - 1)
                        act.activation(sg[0:n, u % 2, 0:w], bank[2 * (u % 2)][0:n, 0:w], ACT.Silu,
                                       scale=gus[0:n, b:b + 1]).then_inc(SC["gate_moved"], 1)
                        u += 1
                for b in range(FB):
                    n = FR[b]
                    act.wait_ge(SC["h_rounded"], b + 1)
                    act.activation(hq[0:n, b, :], hT[0:n, b, :], ACT.Identity, bias=neg_magic_c[0:n]).then_inc(SC["hq"], 1)

            @block.tensor
            def _(pe):
                pe.wait_ge(SC["m_ready"], 1)
                pe.transpose(bank[0][0:1, 0:P], m_col, ident[:, :]).then_inc(SC["m_T"], 1)
                pe.wait_ge(SC["s_row"], 1)
                pe.matmul(bank[1][:, 0:1], ones_m[0:1, :], row[:, 6:7], start=True, stop=True).then_inc(SC["s_bc"], 1)
                for i, (m, b) in enumerate(blocks_w):
                    raw = (raw_g, raw_u)[m]
                    n = FR[b]
                    pe.wait_ge(SC["wq_ready"], i + 1)
                    for j in range(2):
                        f = 2 * i + j
                        if f >= 2:
                            pe.wait_ge(SC["wT_moved"], f - 1)
                        for k in range(4):
                            last = pe.transpose(bank[4 + j][:, k * n:(k + 1) * n], raw[0:n, b, (4 * j + k) * P:(4 * j + k + 1) * P],
                                                ident[0:n, 0:n])
                        last.then_inc(SC["wT_full"], 1)
                pe.wait_ge(SC["wq_ready"], len(blocks_w) + 1)
                for i, b in enumerate(range(FB)):
                    n = FR[b]
                    for j in range(2):
                        f = 2 * (len(blocks_w) + i) + j
                        pe.wait_ge(SC["wT_moved"], f - 1)
                        for k in range(4):
                            last = pe.transpose(bank[4 + j][0:n, k * P:(k + 1) * P], raw_d[:, 4 * j + k, b * P:b * P + n],
                                                ident[:, :])
                        last.then_inc(SC["wT_full"], 1)
                pe.wait_ge(SC["diag"], 1)
                for k in range(K):
                    last = pe.matmul(bank[2 + k // 4][:, (k % 4) * P:(k % 4 + 1) * P], ones_m, diag[:, k, :], start=(k % 4 == 0),
                                     stop=True, skip_group_check=True)
                last.then_inc(SC["drow_full"], 1)

                def xq_tile(t, par, first):
                    pe.wait_ge(SC["q_ready"], t + 1)
                    for j in range(2):
                        if not first:
                            pe.wait_ge(SC["qT_moved"], 2 * t + j - 1)
                        for k in range(4):
                            last = pe.transpose(bank[6 + j][:, k * P:(k + 1) * P], q_t[par][:, 0, (4 * j + k) * P:(4 * j + k + 1) * P],
                                                ident[:, :])
                        last.then_inc(SC["qT_full"], 1)
                xq_tile(0, 0, True)
                xq_tile(1, 1, False)
                with pe.Fori(1, T // 2) as t2:
                    xq_tile(2 * t2, 0, False)
                    xq_tile(2 * t2 + 1, 1, False)
                pe.wait_ge(SC["drow"], 2)
                pe.wait_ge(SC["wT_moved"], 2 * (len(blocks_w) + FB))
                pe.wait_ge(SC["qT_moved"], 2 * T)
                u = 0
                for c, (c0, w) in enumerate(NCH):
                    for b in range(FB):
                        n = FR[b]
                        if u >= 2:
                            pe.wait_ge(SC["gate_moved"], u - 1)
                            pe.wait_ge(SC["up_moved"], u - 1)
                        for m in range(2):
                            for k in range(K):
                                last = pe.matmul(bank[2 * (u % 2) + m][0:n, 0:w], wguT[:, 2 * k + m, b * P:b * P + n],
                                                 xqT[:, k, c0:c0 + w], start=(k == 0), stop=(k == K - 1))
                            last.then_inc(SC["gate_full"], 1)
                        u += 1
                pe.wait_ge(SC["m_ready"], 2)
                pe.transpose(bank[4][0:1, 0:P], m_col, ident[:, :]).then_inc(SC["m_T"], 1)
                pe.wait_ge(SC["s_row"], 2)
                pe.matmul(bank[5][:, 0:1], ones_r[:, :], row[:, 6:7], start=True, stop=True).then_inc(SC["s_bc"], 1)
                pe.wait_ge(SC["hq"], FB)

                def y_tile(t, par, first):
                    for n in range(2):
                        if not first:
                            pe.wait_ge(SC["y_moved"], 2 * t + n - 3)
                        for b in range(FB):
                            r = FR[b]
                            last = pe.matmul(bank[2 * par + n][:, :], hq[0:r, b, bass.ds(t * P, P)],
                                             wdT[0:r, b, n * HALF:(n + 1) * HALF], start=(b == 0), stop=(b == FB - 1))
                        last.then_inc(SC["y_full"], 1)
                y_tile(0, 0, True)
                y_tile(1, 1, True)
                with pe.Fori(1, T // 2) as t2:
                    y_tile(2 * t2, 0, False)
                    y_tile(2 * t2 + 1, 1, False)

            @block.vector
            def _(dve):
                steps = [0]

                def step(ins):
                    steps[0] += 1
                    ins.then_inc(SC["step"], 1)
                    dve.wait_ge(SC["step"], steps[0])

                step(dve.memset(neg_magic_c, -MAGIC))
                step(dve.memset(mh, 0.0))
                step(dve.memset(ones_r[:, :], 1.0))
                step(dve.memset(ones_m, 1.0))

                def scale(i, dst, rdst):
                    dve.wait_ge(SC["m_T"], i + 1)
                    step(dve.tensor_reduce(row[:, 7:8], bank[4 * i][0:1, 0:P], AX.X, ALU.max))
                    if i == 0:
                        dve.wait_ge(SC["exp"], 1)
                    step(dve.tensor_scalar(row[:, 4:5], row[:, 2 + i:3 + i], 1.0, None, ALU.add))
                    step(dve.reciprocal(row[:, 5:6], row[:, 4:5]))
                    step(dve.tensor_tensor(row[:, 7:8], row[:, 7:8], row[:, 5:6], ALU.mult))
                    dve.tensor_scalar(row[:, 6:7], row[:, 7:8], 1.0 / QMAX, None, ALU.mult).then_inc(SC["s_row"], 1)
                    dve.wait_ge(SC["s_bc"], i + 1)
                    step(dve.tensor_copy(dst, bank[4 * i + 1][:, 0:1]))
                    step(dve.reciprocal(rdst, dst))

                step(dve.tensor_reduce(m_col, mx, AX.X, ALU.max))
                dve.nop().then_inc(SC["m_ready"], 1)
                scale(0, s_x, rs_x)

                dve.wait_ge(SC["raw_in"], 16 * 5)

                def weight_scale(i, raw, n):
                    step(dve.tensor_reduce(wsc[0:n, i:i + 1], raw, AX.X, ALU.max, apply_absolute_value=True))
                    step(dve.tensor_scalar(wsc[0:n, i:i + 1], wsc[0:n, i:i + 1], 1.0 / QMAX, None, ALU.mult))
                    step(dve.reciprocal(wrc[0:n, i:i + 1], wsc[0:n, i:i + 1]))
                    step(dve.tensor_scalar(raw, raw, wrc[0:n, i:i + 1], MAGIC, ALU.mult, ALU.add))

                def clamp(a):
                    step(dve.tensor_scalar(a, a, MAGIC + QMAX, MAGIC - QMAX - 1.0, ALU.min, ALU.max))

                for i, (m, b) in enumerate(blocks_w):
                    n = FR[b]
                    raw = (raw_g, raw_u)[m][0:n, b, :]
                    weight_scale(i, raw, n)
                    clamp(raw)
                    dve.nop().then_inc(SC["wq_ready"], 1)
                    step(dve.tensor_scalar(gus[0:n, i:i + 1], wsc[0:n, i:i + 1], s_x[0:n], None, ALU.mult))
                for k in range(K):
                    weight_scale(2 * FB + k, raw_d[:, k, :], P)
                    clamp(raw_d[:, k, :])
                    step(dve.tensor_scalar(diag[:, k, :], ident[:, :], wsc[:, 2 * FB + k:2 * FB + k + 1], None, ALU.mult))
                dve.nop().then_inc(SC["wq_ready"], 1)
                dve.nop().then_inc(SC["diag"], 1)
                dve.wait_ge(SC["drow_full"], 1)
                for j in range(2):
                    dve.tensor_copy(d_row[:, 0, j * HALF:(j + 1) * HALF], bank[2 + j][:, :]).then_inc(SC["drow"], 1)

                def xq_tile(t, par, first):
                    if not first:
                        dve.wait_ge(SC["qT_full"], 2 * t - 2)
                    q = q_t[par][:, 0, :]
                    dve.tensor_scalar(q, xn2[:, bass.ds(t, 1), :].rearrange("p a d -> p (a d)"), rs_x, MAGIC,
                                      ALU.mult, ALU.add).then_inc(SC["q1"], 1)
                    dve.wait_ge(SC["q1"], t + 1)
                    dve.tensor_scalar(q, q, MAGIC + QMAX, MAGIC - QMAX - 1.0, ALU.min, ALU.max).then_inc(SC["q_ready"], 1)
                xq_tile(0, 0, True)
                xq_tile(1, 1, True)
                with dve.Fori(1, T // 2) as t2:
                    xq_tile(2 * t2, 0, False)
                    xq_tile(2 * t2 + 1, 1, False)

                u = 0
                for c, (c0, w) in enumerate(NCH):
                    for b in range(FB):
                        n = FR[b]
                        dve.wait_ge(SC["gate_full"], 2 * u + 2)
                        dve.wait_ge(SC["gate_moved"], u + 1)
                        dve.scalar_tensor_tensor(hT[0:n, b, c0:c0 + w], bank[2 * (u % 2) + 1][0:n, 0:w],
                                                 gus[0:n, FB + b:FB + b + 1], sg[0:n, u % 2, 0:w], ALU.mult,
                                                 ALU.mult).then_inc(SC["up_moved"], 1)
                        dve.wait_ge(SC["up_moved"], u + 1)
                        step(dve.tensor_reduce(mh[0:n, u:u + 1], hT[0:n, b, c0:min(c0 + w, N)], AX.X, ALU.max,
                                               apply_absolute_value=True))
                        u += 1
                step(dve.tensor_reduce(m_col, mh, AX.X, ALU.max))
                dve.nop().then_inc(SC["m_ready"], 1)
                scale(1, s_d, rs_d)
                for b in range(FB):
                    n = FR[b]
                    a = hT[0:n, b, :]
                    step(dve.tensor_scalar(a, a, rs_d[0:n], MAGIC, ALU.mult, ALU.add))
                    dve.tensor_scalar(a, a, MAGIC + QMAX, MAGIC - QMAX - 1.0, ALU.min, ALU.max).then_inc(SC["h_rounded"], 1)

                def y_tile(t, par, t2):
                    dve.wait_ge(SC[f"x2_in{par}"], 16 * t2 + 16)
                    for n in range(2):
                        s = slice(n * HALF, (n + 1) * HALF)
                        dve.wait_ge(SC["y_full"], 2 * t + n + 1)
                        dve.scalar_tensor_tensor(xn2[:, 0, s], bank[2 * par + n][:, :], s_d, d_row[:, 0, s], ALU.mult,
                                                 ALU.mult).then_inc(SC["y_moved"], 1)
                        dve.wait_ge(SC["y_moved"], 2 * t + n + 1)
                        dve.tensor_tensor(x2_c[par][:, 0, s], x2_c[par][:, 0, s], xn2[:, 0, s], ALU.add).then_inc(SC["y_ready"], 1)
                with dve.Fori(0, T // 2) as t2:
                    y_tile(2 * t2, 0, t2)
                    y_tile(2 * t2 + 1, 1, t2)

_INS = ['x', 'src', 'dst', 'L0_gnn_W', 'L0_gnn_b', 'L0_mix_Wq', 'L0_mix_bq', 'L0_mix_Wk', 'L0_mix_bk', 'L0_mix_Wv',
        'L0_mix_bv', 'L0_mix_Wo', 'L0_mix_bo', 'L0_ffn_clip_x', 'L0_ffn_clip_down', 'L0_ffn_w_gate', 'L0_ffn_w_up',
        'L0_ffn_w_down']


def kernel(**inputs):
    import numpy as np
    import concourse.bacc as bacc
    from concourse.bass_utils import run_bass_kernel_spmd

    nc = bacc.Bacc("TRN2", target_bir_lowering=False, num_devices=1)
    arrays, args = {}, []
    for name in _INS:
        a = np.ascontiguousarray(inputs[name])
        arrays[f"in_{name}"] = a
        args.append(nc.dram_tensor(f"in_{name}", a.shape, mybir.dt.from_np(a.dtype), kind="ExternalInput").ap())
    out = nc.dram_tensor("out_x", (N, D), F32, kind="ExternalOutput").ap()
    gps_layer(nc, *args, out)
    r = run_bass_kernel_spmd(nc, [arrays], core_ids=[0])
    return r.results[0]["out_x"]
```

```python
from contextlib import ExitStack

import concourse.bass as bass
from concourse import mybir

ALU = mybir.AluOpType
ACT = mybir.ActivationFunctionType
AX = mybir.AxisListType
F32 = mybir.dt.float32
F16 = mybir.dt.float16
BF16 = mybir.dt.bfloat16
I32 = mybir.dt.int32
U32 = mybir.dt.uint32
U16 = mybir.dt.uint16

P = 128
HALF = 512
N, D = 1250, 1024
T = -(-N // P)
LAST = N - (T - 1) * P
NP = T * P
K = D // P
HEADS, DH = 16, 64
PAIRS = HEADS // 2
E = 40000
EC = 125
C = E // EC
W = 16
WC = W * T
WINDOWS = -(-N // W)
UNITS = 8
COUNTED = T - 2
CU = C // (COUNTED * UNITS)
GROUPS = [(0, 3), (3, 2)]
FF = 352
FB = -(-FF // P)
FR = [min(P, FF - P * b) for b in range(FB)]
QMAX = 127.0
MAGIC = 1.5 * 2.0 ** 23
EPS = 1e-5
EB = [(0, P), (P, P), (2 * P, C - 2 * P)]
NCH = [(0, 512), (512, 512), (1024, 256)]
X_UP = W_UP = 2.0 ** 8
M_UP, H_UP = 2.0 ** 8, 2.0 ** 4
COUNT_MAX = 2048
ROUNDS = -(-(E + 1) // COUNT_MAX)
assert E == EC * C and CU * COUNTED * UNITS == C and T == 10


def gps_layer(nc, x, src, dst, gnn_W, gnn_b, Wq, bq, Wk, bk, Wv, bv, Wo, bo,
              clip_x, clip_down, w_gate, w_up, w_down, out):
    with ExitStack() as ctx:
        def sb(name, shape, dt):
            return ctx.enter_context(nc.sbuf_tensor(name, shape, dt))

        def sems(*names):
            return {n: ctx.enter_context(nc.semaphore(n)) for n in names}

        bank = [ctx.enter_context(nc.psum_tensor(f"bank{i}", [P, HALF], F32)) for i in range(8)]
        proj, kv_acc, tp, agg = bank[0:2], bank[2:4], bank[4:6], bank[6:8]

        qT_d = nc.dram_tensor("qT_d", [T, P, 2 * D], F16, kind="Internal").ap()
        g_d = nc.dram_tensor("g_d", [T, P, D], F32, kind="Internal").ap()

        SLOT = K * HALF
        mem = sb("mem", [P, 8 * SLOT + 11 * D], F32)

        def part(at, *dims, dt=F32):
            size = 1
            for d in dims:
                size *= d
            words = size * (2 if dt in (F16, BF16) else 4) // 4
            a = mem[:, at:at + words]
            if dt != F32:
                a = a.bitcast(dt)
            if len(dims) == 2:
                a = a.rearrange("p (a b) -> p a b", b=dims[1])
            if len(dims) == 3:
                a = a.rearrange("p (a b c) -> p a b c", b=dims[1], c=dims[2])
            return a

        w_raw = [part((i + 1) * SLOT, K, HALF) for i in range(8)]
        w16 = [part(i * SLOT, K, 2, HALF, dt=F16) for i in range(8)]
        S8 = 8 * SLOT
        qT_o = part(S8 + D, 2, K * P, dt=F16)
        g_o = part(S8 + 2 * D, D)
        xT = [part(S8 + 4 * D, 2, K, P, dt=F16), part(S8 + 3 * D, 2, K, P, dt=F16)]
        x_in, k_t, v_t, q_t, bk_b, bv_b = [part(S8 + (5 + i) * D, D) for i in range(6)]
        e_src, e_dst = [part(S8 + 8 * D + 3 * EC * i, 3, EC) for i in range(2)]
        e_tmp = part(S8 + 8 * D + 6 * EC, EC)
        sources = part(S8 + 4 * D, NP)
        kvs = part(S8, PAIRS, P)
        wo = part(0, K, D)
        m16 = [part(2 * SLOT + i * SLOT, K, D, dt=F16) for i in range(2)]
        H0 = 4 * SLOT
        h16 = part(H0, T, 2 * D, dt=F16)
        x2 = part(H0 + T * D, T, D)
        a_t = part(S8 + 4 * D, T, P, dt=F16)
        x_t = [x_in, v_t]
        g_in = [k_t, v_t]
        qT_i, bo_b, gb_b = q_t.bitcast(F16).rearrange("p (a b c) -> p a b c", a=2, b=K), bk_b, bv_b
        raw = [part(i * D, D) for i in range(2)]
        at = 2 * D
        wguT = part(at, K * 2, FF, dt=BF16)
        at += K * FF
        wdT = part(at, FB, D, dt=BF16)
        at += FB * D // 2
        d_row = part(at, D)
        at += D
        ones_m = part(at, P)
        diag = part(at + P, 2, P)
        assert at + 3 * P <= 2 * SLOT
        C0 = 2 * SLOT
        xqT = part(C0, K, NP, dt=BF16)
        C0 += K * NP // 2
        sg = part(C0, 2, HALF)
        q_c = [part(C0 + D + i * D, D) for i in range(2)]
        assert C0 + 3 * D <= H0
        hT = part(H0, FB, NP)
        hq = part(H0 + FB * NP, FB, NP, dt=BF16)
        y_t = part(H0 + FB * NP * 3 // 2, D)
        assert FB * NP * 3 // 2 + D <= T * D

        counts = sb("counts", [P, NP * T], U16)
        keyT = sb("keyT", [P, C + CU], F32)
        loT = sb("loT", [P, C], F32)
        base_row = sb("base_row", [1, C], I32)
        iota_w = sb("iota_w", [P, WC], BF16)
        iota_p = sb("iota_p", [P, P], BF16)
        hot_dst = sb("hot_dst", [P, CU, WC], BF16)
        hot_src = sb("hot_src", [P, 2, CU, P], BF16)
        src_col = sb("src_col", [P, 2, CU], F32)
        ident = sb("ident", [P, P], F32)
        stats = sb("stats", [P, 2, 6], F32)
        cols = sb("cols", [P, 160], F32)
        col_at = [0]

        def col(n=1):
            col_at[0] += n
            return cols[:, col_at[0] - n:col_at[0]]

        mv, var_eps, exponent, rstd = col(2), col(), col(), col()
        half_neg, dinv, dinv_up, dinv_down = col(T), col(T), col(T), col(T)
        ln_mean, ln_rstd, mx, m_col, ones, neg_magic = col(T), col(T), col(T), col(), col(), col()
        s_x, rs_x, s_d, rs_d = col(), col(), col(), col()
        e_min, e_span, most_c = col(4), col(4), col(T // 2)
        wsc, wrc, gus, mh = col(2 * FB + K), col(2 * FB + K), col(2 * FB), col(9)
        bq_rows, bq_c = sb("bq_rows", [K, P], F32), sb("bq_c", [P, K], F32)
        row = sb("row", [1, 8], F32)
        flags = sb("flags", [1, 2], I32)
        ones_r = sb("ones_r", [1, P], F32)

        S = sems("consts", "pool_step", "edges_in", "bias_in", *[f"w_in{i}" for i in range(8)], "x_in", "dve_step",
                 "ln_step", "var_ready", "rstd_ready", "edges_ready", "edges_T", "columns", "ln_done", "tp_full",
                 "fill_hi", "fill_lo", "unit_full", "dve_evac", "act_evac", "k_relu", "q_relu", "kv_done",
                 "qT_stored", "g_stored", "w_hi", "w_lo", "hot_dst_ready", "src_col_ready", "hot_src_ready", "adj_mm",
                 "adj_added", "counts_set")
        SE = sems("e_hot", "e_mm")
        SM = sems("wo_in", "b_bias_in", "g_in0", "g_in1", "kvs", "sources", "deg_full", "deg_ready", "dinv", "prod_full",
                  "m_hi", "m_lo", "h_hi", "h_lo", "max_col", "max_T")
        SB = sems("qT_in", "xb_in0", "xb_in1", "x_bias", "a_ready", "mix_full", "agg_full", "mix_moved", "agg_moved",
                  "x2_step", "b_var", "b_rstd", "b_norm", "b_max", "a_more", "a_more_used")
        SF = sems("raw_in0", "raw_in1", "wq_ready", "wT_full", "wT_moved", "diag", "drow_full", "drow")
        SC = sems("clip_in", "c_step", "m_ready", "m_T", "s_row", "s_bc", "exp", "xn", "q1", "q_ready", "qT_full",
                  "qT_moved", "gate_full", "silu", "up_moved", "h_rounded", "hq", "y_full", "y_moved", "y_ready", "stored")

        def over_tiles(eng, tile):
            tile(0, 0, 0)
            tile(1, 1, 0)
            with eng.Fori(1, T // 2 - 1) as t2:
                for par in range(2):
                    tile(2 * t2 + par, par, t2)
            tile(T - 2, 0, T // 2 - 1)
            tile(T - 1, 1, T // 2 - 1)

        def counted_tiles(eng, tile):
            tile(1, 1, True)
            tile(2, 0, False)
            with eng.Fori(1, COUNTED // 2) as t2:
                tile(2 * t2 + 1, 1, False)
                tile(2 * t2 + 2, 0, False)

        pieces = [("gu", m, b) for m in range(2) for b in range(FB)] + [("down", k, 0) for k in range(0, K, 2)]
        slots = [(0, 1), (0, 2), (0, 3), (1, 0), (1, 1), (1, 2), (1, 3), (T - 2, 0), (T - 2, 1), (T - 2, 2)]
        fills_of = [2 if kind == "gu" else FB for kind, _, _ in pieces]

        TILES_OF = [range(c0 // P, (c0 + w) // P) for c0, w in NCH]
        FFN_ORDER = [("quantise", 0), ("quantise", 1), ("products", 0), ("quantise", 2), ("products", 1), ("products", 2)]

        block = ctx.enter_context(nc.Block())


        @block.sync
        def _(sp):
            halves = [(w, h) for w in (Wk, Wv, Wq, gnn_W) for h in range(2)]

            def load_half(i):
                w, h = halves[i]
                sp.dma_start(w_raw[i], w.rearrange("(k p) n -> p k n", p=P)[:, :, h * HALF:(h + 1) * HALF]).then_inc(S[f"w_in{i}"], 16)

            sp.dma_start(x_in, x[0:P, :]).then_inc(S["x_in"], 16)
            load_half(0)
            for e, a in ((e_dst.bitcast(I32), dst), (e_src.bitcast(I32), src)):
                ev = a.rearrange("(c e) -> c e", e=EC)
                sp.dma_start(e[:, 0:2, 0:EC], ev[0:2 * P].rearrange("(b p) e -> p b e", p=P)).then_inc(S["edges_in"], 16)
                sp.dma_start(e[0:EB[2][1], 2, 0:EC], ev[2 * P:C]).then_inc(S["edges_in"], 16)
            for b_sb, b in ((bk_b, bk), (bv_b, bv)):
                sp.dma_start(b_sb, b.rearrange("(a n) -> a n", a=1).broadcast_to([P, D])).then_inc(S["bias_in"], 16)
            sp.dma_start(bq_rows[:, :], bq.rearrange("(k p) -> k p", p=P)).then_inc(S["bias_in"], 16)
            for i in range(1, 8):
                load_half(i)
            sp.wait_ge(S["tp_full"], 2)
            sp.dma_start(x_in, x[P:2 * P, :]).then_inc(S["x_in"], 16)

            def store_g(t):
                sp.wait_ge(S["act_evac"], 4 * t + 4)
                sp.dma_start(g_d[bass.ds(t, 1)].rearrange("a p d -> (a p) d"), g_o).then_inc(S["g_stored"], 16)

            def store_q(t, last_tile=False):
                sp.wait_ge(S["fill_lo"], 40 if last_tile else 4 * t + 6)
                sp.dma_start(qT_d[bass.ds(t, 1)].rearrange("a p d -> (a p) d"),
                             qT_o.rearrange("p a b -> p (a b)")).then_inc(S["qT_stored"], 16)

            with sp.Fori(0, T - 3) as t:
                sp.wait_ge(S["tp_full"], 4 * t + 4)
                sp.dma_start(x_in, x[bass.ds((t + 2) * P, P), :]).then_inc(S["x_in"], 16)
                store_g(t)
                store_q(t)
            sp.wait_ge(S["tp_full"], 4 * (T - 3) + 4)
            sp.dma_start(x_in[0:LAST, :], x[(T - 1) * P:N, :]).then_inc(S["x_in"], 16)
            for t in (T - 3, T - 2):
                store_g(t)
                store_q(t)

            sp.wait_ge(SM["deg_full"], 1)
            sp.dma_start(x_t[0], x[0:P, :]).then_inc(SB["xb_in0"], 16)
            sp.wait_ge(S["unit_full"], UNITS * (T - 1) + 2)
            sp.dma_start(wo, Wo.rearrange("(k p) n -> p k n", p=P)).then_inc(SM["wo_in"], 16)
            sp.wait_ge(S["dve_evac"], 4 * T)
            for b_sb, b in ((bo_b, bo), (gb_b, gnn_b)):
                sp.dma_start(b_sb, b.rearrange("(a n) -> a n", a=1).broadcast_to([P, D])).then_inc(SM["b_bias_in"], 16)

            def load_g(t):
                if t >= 2:
                    sp.wait_ge(SM["h_lo"], t - 1)
                sp.dma_start(g_in[t % 2], g_d[t]).then_inc(SM[f"g_in{t % 2}"], 16)

            sp.wait_ge(S["kv_done"], T)
            sp.wait_ge(S["g_stored"], 16 * (T - 1))
            load_g(0)
            load_g(1)
            store_g(T - 1)
            for t in range(2, T - 1):
                load_g(t)
            sp.wait_ge(S["g_stored"], 16 * T)
            load_g(T - 1)
            store_q(T - 1, True)
            sp.wait_ge(S["qT_stored"], 16 * T)

            def load_q(t):
                sp.dma_start(qT_i.rearrange("p a b c -> p (a b c)"), qT_d[bass.ds(t, 1)].rearrange("a p d -> (a p) d")).then_inc(SB["qT_in"], 16)

            load_q(0)
            sp.wait_ge(SM["h_lo"], T)
            sp.dma_start(x_t[1], x[P:2 * P, :]).then_inc(SB["xb_in1"], 16)

            def load_piece(i):
                kind, a, b = pieces[i]
                if i < 2:
                    sp.wait_ge(SM["prod_full"], 2 * PAIRS)
                else:
                    sp.wait_ge(SF["wT_full"], sum(fills_of[:i - 1]))
                if kind == "gu":
                    sp.dma_start(raw[i % 2][0:FR[b], :], (w_gate, w_up)[a][b * P:b * P + FR[b], :]).then_inc(SF[f"raw_in{i % 2}"], 16)
                else:
                    sp.dma_start(raw[i % 2][:, 0:2 * FF].rearrange("p (k i) -> p k i", i=FF),
                                 w_down[a * P:(a + 2) * P, :].rearrange("(k p) i -> p k i", p=P)).then_inc(SF[f"raw_in{i % 2}"], 16)

            LOADS = {0: range(2, 7), 1: range(7, 9), T - 2: range(9, 10)}
            load_piece(0)
            load_piece(1)

            def tile(t, par, t2):
                fixed = isinstance(t, int)
                if not (fixed and t == T - 1):
                    sp.wait_ge(SB["mix_full"], 2 * t + 2)
                    load_q(t + 1)
                if fixed and t in LOADS:
                    for i in LOADS[t]:
                        load_piece(i)
                if not (fixed and t >= T - 2):
                    sp.wait_ge(SB["b_max"], t + 1)
                    rows = LAST if fixed and t == T - 3 else P
                    sp.dma_start(x_t[par][0:rows, :], x[bass.ds(P * t + 2 * P, rows), :]).then_inc(SB[f"xb_in{par}"], 16)

            tile(0, 0, 0)
            tile(1, 1, 0)
            with sp.Fori(1, T // 2 - 2) as t2:
                for par in range(2):
                    tile(2 * t2 + par, par, t2)
            for t in range(T - 4, T):
                tile(t, t % 2, t // 2)

            sp.dma_start(row[:, 0:1], clip_x.rearrange("(a n) -> a n", a=1)).then_inc(SC["clip_in"], 16)
            sp.dma_start(row[:, 1:2], clip_down.rearrange("(a n) -> a n", a=1)).then_inc(SC["clip_in"], 16)

            def store_out(t, rows):
                sp.wait_ge(SC["y_ready"], 2 * t + 2)
                sp.dma_start(out[bass.ds(P * t, rows), :],
                             x2[0:rows, bass.ds(t, 1), :].rearrange("p a d -> p (a d)")).then_inc(SC["stored"], 16)
            with sp.Fori(0, T - 1) as t:
                store_out(t, P)
            store_out(T - 1, LAST)
            sp.wait_ge(SC["stored"], 16 * T)


        @block.gpsimd
        def _(pool):
            pool.memset(ident[:, :], 0.0).then_inc(S["pool_step"], 1)
            pool.memset(counts[:, :].bitcast(U32), 0).then_inc(S["counts_set"], 1)
            pool.wait_ge(S["pool_step"], 1)
            pool.affine_select(out=ident[:, :], in_=ident[:, :], compare_op=ALU.not_equal, fill=1.0, base=0,
                               pattern=[[-1, P]], channel_multiplier=1).then_inc(S["consts"], 1)
            pool.iota(iota_w[:, :], [[1, WC]], base=0, channel_multiplier=0,
                      allow_small_or_imprecise_dtypes=True).then_inc(S["consts"], 1)
            pool.iota(iota_p[:, :], [[1, P]], base=0, channel_multiplier=0,
                      allow_small_or_imprecise_dtypes=True).then_inc(S["consts"], 1)

            def inverse_deviation(n):
                pool.wait_ge(S["var_ready"], n + 1)
                pool.tensor_tensor(rstd, var_eps, exponent, ALU.pow).then_inc(S["rstd_ready"], 1)

            inverse_deviation(0)
            inverse_deviation(1)
            pool.wait_ge(S["columns"], 2)
            pool.wait_ge(S["consts"], 3)

            def tile(t, par, first):
                for j in range(UNITS):
                    u = UNITS * (t - 1) + j
                    if not (first and j < 2):
                        pool.wait_ge(S["adj_mm"], 2 * u - 2)
                    pool.tensor_copy(src_col[0:EC, j % 2, :], loT[0:EC, bass.ds(u * CU, CU)]).then_inc(S["src_col_ready"], 1)
                    pool.drain()
                    for i in range(CU):
                        pool.tensor_scalar(hot_src[0:EC, j % 2, i, :], iota_p[0:EC, :], src_col[0:EC, j % 2, i:i + 1],
                                           None, ALU.is_equal).then_inc(S["hot_src_ready"], 1)
                    if j == 3:
                        inverse_deviation(t + 1)

            counted_tiles(pool, tile)

            pool.wait_ge(SM["deg_ready"], 1)
            pool.tensor_tensor(dinv, dinv, half_neg, ALU.pow).then_inc(SM["dinv"], 1)
            pool.wait_ge(SM["dinv"], 1)
            pool.tensor_scalar(dinv_up, dinv, H_UP, None, ALU.mult).then_inc(SM["dinv"], 1)
            pool.tensor_scalar(dinv_down, dinv, 1.0 / H_UP, None, ALU.mult).then_inc(SM["dinv"], 1)

            pool.wait_ge(SM["b_bias_in"], 32)

            def tile_b(t, par, t2):
                pool.wait_ge(SB[f"xb_in{par}"], 16 * t2 + 16)
                pool.tensor_tensor(x_t[par], x_t[par], bo_b, ALU.add).then_inc(SB["x_bias"], 1)
                pool.wait_ge(SB["b_var"], t + 1)
                pool.tensor_tensor(rstd, var_eps, exponent, ALU.pow).then_inc(SB["b_rstd"], 1)

            over_tiles(pool, tile_b)


        @block.tensor
        def _(pe):
            def transposes(source, f, first=False):
                for j in range(2):
                    if not first:
                        pe.wait_ge(S["fill_lo"], f + j - 1)
                        pe.wait_ge(S["fill_hi"], f + j - 1)
                    for k in range(4):
                        last = pe.transpose(tp[j][:, k * P:(k + 1) * P],
                                            source[:, (4 * j + k) * P:(4 * j + k + 1) * P], ident[:, :])
                    last.then_inc(S["tp_full"], 1)

            def count_group(u, i, par, first):
                c0, n = GROUPS[i]
                pe.wait_ge(S["hot_src_ready"], CU * u + CU)
                pe.wait_ge(S["hot_dst_ready"], CU * u + c0 + n)
                if not first:
                    pe.wait_ge(S["adj_added"], CU * (u - 1) + c0 + n)
                for cc in range(n):
                    last = pe.matmul(agg[i][:, cc * WC:(cc + 1) * WC], hot_src[0:EC, par, c0 + cc, :],
                                     hot_dst[0:EC, c0 + cc, :], start=(cc == 0), stop=True, skip_group_check=True)
                last.then_inc(S["adj_mm"], 1)

            pe.wait_ge(S["consts"], 1)
            pe.wait_ge(S["ln_done"], 1)
            transposes(x_in, 0, True)

            def tile(t, par, counting=True, first_counted=False):
                first, last_tile = isinstance(t, int) and t == 0, isinstance(t, int) and t == T - 1
                for j in range(UNITS):
                    half = j % 2
                    if j == 0:
                        pe.wait_ge(S["fill_lo"], 2 if first else 4 * t)
                    if j < 2:
                        if not first:
                            pe.wait_ge(S["act_evac"], 4 * t - 1 + j)
                    elif j < 6:
                        pe.wait_ge(S["dve_evac"], 4 * t + j - 1)
                    else:
                        pe.wait_ge(S["act_evac"], 4 * t + j - 5)
                    for k in range(K):
                        if first and k % 4 == 0:
                            pe.wait_ge(S["w_lo"], 2 * j + k // 4 + 1)
                        for a, b in ((0, 0), (0, 1), (1, 0)):
                            last = pe.matmul(proj[half][:, :], xT[par][:, a, k, :], w16[j][:, k, b, :],
                                             start=(k == 0 and a == b), stop=(k == K - 1 and a == 1))
                        if k == K - 1:
                            last.then_inc(S["unit_full"], 1)
                        if counting and k % 4 == 3:
                            count_group(UNITS * (t - 1) + j, k // 4, j % 2, first_counted and j == 0)
                    if first and j == 3:
                        edge_columns()
                    if j == (7 if first else 3) and not last_tile:
                        pe.wait_ge(S["ln_done"], t + 2)
                        transposes(x_in, 4 * t + 2)
                    if j == 4:
                        rows = LAST if last_tile else P
                        pe.wait_ge(S["k_relu"], 2 * t + 2)
                        pe.wait_ge(S["dve_evac"], 4 * t + 4)
                        for p in range(PAIRS):
                            o = kv_acc[p // 4][:, (p % 4) * P:(p % 4 + 1) * P]
                            last = pe.matmul(o, v_t[0:rows, p * P:(p + 1) * P], k_t[0:rows, p * P:(p + 1) * P],
                                             start=(first and p % 4 == 0), stop=last_tile, skip_group_check=True)
                        last.then_inc(S["kv_done"], 1)
                    if last_tile and j == 6:
                        degrees()
                pe.wait_ge(S["act_evac"], 4 * t + 2)
                transposes(q_t, 4 * t + (2 if last_tile else 4))

            def edge_columns():
                pe.wait_ge(S["edges_ready"], 1)
                for b, (c0, n) in enumerate(EB):
                    pe.transpose(agg[0][0:EC, c0:c0 + n], e_dst[0:n, b, :], ident[0:n, 0:n])
                    pe.transpose(agg[1][0:EC, c0:c0 + n], e_src[0:n, b, :], ident[0:n, 0:n])
                    pe.transpose(tp[0][0:1, c0:c0 + n], e_min[0:n, b:b + 1], ident[0:n, 0:n])
                    pe.transpose(tp[1][0:1, c0:c0 + n], e_span[0:n, b:b + 1], ident[0:n, 0:n])
                pe.wait_ge(S["bias_in"], 48)
                pe.transpose(tp[0][:, C:C + K], bq_rows[:, :], ident[0:K, 0:K]).then_inc(S["edges_T"], 1)
                pe.wait_ge(S["columns"], 5)

            def degrees():
                pe.wait_ge(SM["sources"], 1)
                for n in range(T):
                    last = pe.matmul(agg[0][:, n:n + 1], sources[:, n * P:(n + 1) * P], ones, start=True, stop=True,
                                     skip_group_check=True)
                last.then_inc(SM["deg_full"], 1)
                pe.wait_ge(SM["max_col"], 1)
                pe.transpose(agg[1][0:1, 0:P], m_col, ident[:, :]).then_inc(SM["max_T"], 1)

            tile(0, 0, False)
            counted_tiles(pe, lambda t, par, first: tile(t, par, True, first))

            pe.wait_ge(S["adj_added"], C)
            span = pe.value_load(flags[0:1, 0:1], min_val=0, max_val=N)
            with pe.If(span >= W):
                with pe.Fori(1, WINDOWS) as k:
                    with pe.Fori(0, C) as c:
                        pe.wait_ge(SE["e_hot"], 2 * ((k - 1) * C + c) + 2)
                        pe.matmul(agg[0][:, 0:WC], hot_src[0:EC, 0, 0, :], hot_dst[0:EC, 0, :], start=True,
                                  stop=True).then_inc(SE["e_mm"], 1)
            tile(T - 1, 1, False)

            pe.wait_ge(SM["kvs"], 4)
            pe.wait_ge(SM["wo_in"], 16)
            for i in range(2 * PAIRS):
                p, n = i // 2, i % 2
                if i >= 2:
                    pe.wait_ge(SM["m_lo"], i - 1)
                else:
                    pe.wait_ge(S["act_evac"], 4 * T)
                pe.matmul(proj[n][:, :], kvs[:, p, :], wo[:, p, n * HALF:(n + 1) * HALF], start=True,
                          stop=True).then_inc(SM["prod_full"], 1)

            fill = [0]

            def piece(i):
                kind, a, b = pieces[i]
                pe.wait_ge(SF["wq_ready"], i + 1)
                for j in range(fills_of[i]):
                    f = fill[0]
                    if f >= 2:
                        pe.wait_ge(SF["wT_moved"], f - 1)
                    else:
                        pe.wait_ge(S["fill_lo"], 4 * T)
                    o = tp[f % 2]
                    if kind == "gu":
                        n = FR[b]
                        for k in range(4):
                            last = pe.transpose(o[:, k * n:(k + 1) * n], raw[i % 2][0:n, (4 * j + k) * P:(4 * j + k + 1) * P],
                                                ident[0:n, 0:n])
                    else:
                        n = FR[j]
                        for k in range(2):
                            last = pe.transpose(o[0:n, k * P:(k + 1) * P], raw[i % 2][:, k * FF + j * P:k * FF + j * P + n],
                                                ident[:, :])
                    last.then_inc(SF["wT_full"], 1)
                    fill[0] += 1
                if kind == "down":
                    for k in range(2):
                        kk = a + k
                        pe.wait_ge(SF["diag"], kk + 1)
                        pe.matmul(kv_acc[kk // 4][:, (kk % 4) * P:(kk % 4 + 1) * P], ones_m, diag[:, kk % 2, :],
                                  start=(kk % 4 == 0), stop=True, skip_group_check=True).then_inc(SF["drow_full"], 1)

            agg_matmuls = [(s, b) for s in range(T) for b in range(2)]

            def tile_b(t, par, t2):
                fixed = isinstance(t, int)
                pe.wait_ge(SB["qT_in"], 16 * t + 16)
                for n in range(2):
                    if fixed and t == 0:
                        pe.wait_ge(SM["m_lo"], 2 * PAIRS)
                    else:
                        pe.wait_ge(SB["mix_moved"], 2 * t - 1 + n)
                    for k in range(K):
                        for a, b in ((0, 0), (0, 1), (1, 0)):
                            last = pe.matmul(proj[n][:, :], qT_i[:, a, k, :], m16[b][:, k, n * HALF:(n + 1) * HALF],
                                             start=(k == 0 and a == b), stop=(k == K - 1 and a == 1))
                    last.then_inc(SB["mix_full"], 1)
                    if fixed and (t, n) in slots:
                        piece(slots.index((t, n)))
                if fixed and t == 0:
                    pe.wait_ge(SM["h_lo"], T)

                def aggregate(n, fresh):
                    for s, b in agg_matmuls:
                        last = pe.matmul(agg[n][:, :], a_t[:, s, :], h16[:, s, b * D + n * HALF:b * D + (n + 1) * HALF],
                                         start=(fresh and s == 0 and b == 0), stop=(s == T - 1 and b == 1),
                                         skip_group_check=True)
                    return last

                for n in range(2):
                    if not (fixed and t == 0):
                        pe.wait_ge(SB["agg_moved"], 2 * t - 1 + n)
                pe.wait_ge(SB["a_ready"], t + 1)
                for n in range(2):
                    aggregate(n, True).then_inc(SB["agg_full"], 1)
                with pe.If(most > COUNT_MAX):
                    with pe.Fori(0, ROUNDS - 1) as r:
                        pe.wait_ge(SB["a_more"], t * (ROUNDS - 1) + r + 1)
                        aggregate(0, False)
                        aggregate(1, False).then_inc(SB["a_more_used"], 1)
                for n in range(2):
                    if fixed and (t, 2 + n) in slots:
                        piece(slots.index((t, 2 + n)))

            pe.wait_ge(SM["max_col"], 2)
            most = pe.value_load(flags[0:1, 1:2], min_val=0, max_val=E + 1)
            over_tiles(pe, tile_b)

            def broadcast(i, b):
                pe.wait_ge(SC["m_ready"], i + 1)
                pe.transpose(bank[b][0:1, 0:P], m_col, ident[:, :]).then_inc(SC["m_T"], 1)
                pe.wait_ge(SC["s_row"], i + 1)
                pe.matmul(bank[b + 1][:, 0:1], ones_r[:, :], row[:, 6:7], start=True, stop=True).then_inc(SC["s_bc"], 1)

            broadcast(0, 2)

            def xq_tile(t, par, first=False):
                pe.wait_ge(SC["q_ready"], t + 1)
                for j in range(2):
                    if not first:
                        pe.wait_ge(SC["qT_moved"], 2 * t + j - 1)
                    for k in range(4):
                        last = pe.transpose(tp[j][:, k * P:(k + 1) * P], q_c[par][:, (4 * j + k) * P:(4 * j + k + 1) * P],
                                            ident[:, :])
                    last.then_inc(SC["qT_full"], 1)

            def gate_up(c):
                c0, w = NCH[c]
                for b in range(FB):
                    u, n = FB * c + b, FR[b]
                    pair = (bank[0:2], bank[6:8])[u % 2]
                    if u >= 2:
                        pe.wait_ge(SC["silu"], u - 1)
                        pe.wait_ge(SC["up_moved"], u - 1)
                    for m in range(2):
                        for k in range(K):
                            last = pe.matmul(pair[m][0:n, 0:w], wguT[:, 2 * k + m, b * P:b * P + n],
                                             xqT[:, k, c0:c0 + w], start=(k == 0), stop=(k == K - 1))
                        last.then_inc(SC["gate_full"], 1)

            for what, c in FFN_ORDER:
                if what == "quantise":
                    for t in TILES_OF[c]:
                        xq_tile(t, t % 2, t == 0)
                else:
                    pe.wait_ge(SC["qT_moved"], 2 * (TILES_OF[c][-1] + 1))
                    gate_up(c)
            broadcast(1, 2)
            pe.wait_ge(SC["hq"], FB)

            def y_tile(t, par, first=False):
                for n in range(2):
                    if not first:
                        pe.wait_ge(SC["y_moved"], 2 * t + n - 3)
                    for b in range(FB):
                        r = FR[b]
                        last = pe.matmul(bank[2 * par + n + (4 if par else 0)][:, :], hq[0:r, b, bass.ds(t * P, P)],
                                         wdT[0:r, b, n * HALF:(n + 1) * HALF], start=(b == 0), stop=(b == FB - 1))
                    last.then_inc(SC["y_full"], 1)
            y_tile(0, 0, True)
            y_tile(1, 1, True)
            with pe.Fori(1, T // 2) as t2:
                y_tile(2 * t2, 0)
                y_tile(2 * t2 + 1, 1)


        @block.scalar
        def _(act):
            def high(f, j, dst_ap, scale):
                act.activation(dst_ap, tp[j][:, :], ACT.Copy, scale=scale).then_inc(S["fill_hi"], 1)

            def xT_fill(f, par):
                for j in range(2):
                    act.wait_ge(S["tp_full"], f + j + 1)
                    high(f, j, xT[par][:, 0, 4 * j:4 * j + 4, :].rearrange("p k n -> p (k n)"), X_UP)

            def weight_high(i):
                act.wait_ge(S[f"w_in{i}"], 16)
                for c in range(2):
                    if i > 0:
                        act.wait_ge(S["w_lo"], 2 * i - 1 + c)
                    act.activation(w16[i][:, 4 * c:4 * c + 4, 0, :], w_raw[i][:, 4 * c:4 * c + 4, :], ACT.Copy,
                                   scale=W_UP).then_inc(S["w_hi"], 1)

            def q_evac(t, h):
                act.wait_ge(S["unit_full"], UNITS * t + 5 + h)
                if h == 0 and not (isinstance(t, int) and t == 0):
                    act.wait_ge(S["tp_full"], 4 * t + 2)
                act.activation(q_t[:, h * HALF:(h + 1) * HALF], proj[h][:, :], ACT.Copy,
                               scale=1.0 / (X_UP * W_UP)).then_inc(S["act_evac"], 1)

            def g_evac(t, h):
                act.wait_ge(S["unit_full"], UNITS * t + 7 + h)
                if h == 0 and not (isinstance(t, int) and t == 0):
                    act.wait_ge(S["g_stored"], 16 * t)
                act.activation(g_o[:, h * HALF:(h + 1) * HALF], proj[h][:, :], ACT.Copy,
                               scale=1.0 / (X_UP * W_UP)).then_inc(S["act_evac"], 1)

            def relu_k(t, h):
                act.wait_ge(S["dve_evac"], 4 * t + 1 + h)
                kh = k_t[:, h * HALF:(h + 1) * HALF]
                act.activation(kh, kh, ACT.Relu).then_inc(S["k_relu"], 1)

            def qT_fill(t, f):
                if not (isinstance(t, int) and t == 0):
                    act.wait_ge(S["qT_stored"], 16 * t)
                for j in range(2):
                    act.wait_ge(S["tp_full"], f + j + 1)
                    for k in range(4):
                        o = tp[j][:, k * P:(k + 1) * P]
                        act.activation(o, o, ACT.Relu, bias=bq_c[:, 4 * j + k:4 * j + k + 1]).then_inc(S["q_relu"], 1)
                    act.wait_ge(S["q_relu"], 8 * t + 4 * j + 4)
                    high(f, j, qT_o[:, 0, j * HALF:(j + 1) * HALF], 1.0)

            xT_fill(0, 0)
            for i in range(4):
                weight_high(i)
            relu_k(0, 0)
            weight_high(4)
            relu_k(0, 1)
            weight_high(5)
            weight_high(6)
            q_evac(0, 0)
            weight_high(7)
            q_evac(0, 1)
            act.wait_ge(S["w_lo"], 16)
            g_evac(0, 0)
            g_evac(0, 1)
            xT_fill(2, 1)
            act.wait_ge(S["columns"], 5)
            qT_fill(0, 4)

            def tile(t, par, last_tile=False):
                for h in range(2):
                    relu_k(t, h)
                if not last_tile:
                    xT_fill(4 * t + 2, 1 - par)
                for h in range(2):
                    q_evac(t, h)
                for h in range(2):
                    g_evac(t, h)
                qT_fill(t, 4 * t + (2 if last_tile else 4))

            counted_tiles(act, lambda t, par, first: tile(t, par))
            tile(T - 1, 1, True)

            act.wait_ge(SM["dinv"], 3)
            act.wait_ge(S["unit_full"], UNITS * T)
            for i in range(2 * PAIRS):
                act.wait_ge(SM["prod_full"], i + 1)
                act.activation(m16[0][:, i // 2, (i % 2) * HALF:(i % 2 + 1) * HALF], proj[i % 2][:, :],
                               ACT.Copy).then_inc(SM["m_hi"], 1)
            for t in range(T):
                act.wait_ge(SM[f"g_in{t % 2}"], 16 * (t // 2 + 1))
                act.activation(h16[:, t, 0:D], g_in[t % 2], ACT.Copy, scale=dinv_up[:, t:t + 1]).then_inc(SM["h_hi"], 1)

            f = 0
            act.wait_ge(SC["c_step"], 1)
            for i, (kind, a, b) in enumerate(pieces):
                for j in range(fills_of[i]):
                    act.wait_ge(SF["wT_full"], f + 1)
                    if kind == "gu":
                        n = FR[b]
                        act.activation(wguT.rearrange("p (k m) f -> p k m f", m=2)[:, 4 * j:4 * j + 4, a, b * P:b * P + n],
                                       tp[f % 2][:, 0:4 * n].rearrange("p (k n) -> p k n", n=n), ACT.Identity,
                                       bias=neg_magic).then_inc(SF["wT_moved"], 1)
                    else:
                        n = FR[j]
                        act.activation(wdT[0:n, j, a * P:(a + 2) * P], tp[f % 2][0:n, 0:2 * P], ACT.Identity,
                                       bias=neg_magic[0:n]).then_inc(SF["wT_moved"], 1)
                    f += 1

            act.wait_ge(SC["clip_in"], 32)
            act.activation(row[:, 2:4], row[:, 0:2], ACT.Exp, scale=-1.0).then_inc(SC["exp"], 1)

            def xq_tile(t):
                for j in range(2):
                    act.wait_ge(SC["qT_full"], 2 * t + j + 1)
                    act.activation(xqT[:, 4 * j:4 * j + 4, bass.ds(t * P, P)],
                                   tp[j][:, :].rearrange("p (k n) -> p k n", n=P), ACT.Identity,
                                   bias=neg_magic).then_inc(SC["qT_moved"], 1)

            for what, c in FFN_ORDER:
                if what == "quantise":
                    with act.Fori(TILES_OF[c][0], TILES_OF[c][-1] + 1) as t:
                        xq_tile(t)
                    continue
                w = NCH[c][1]
                for b in range(FB):
                    u, n = FB * c + b, FR[b]
                    act.wait_ge(SC["gate_full"], 2 * u + 1)
                    if u >= 2:
                        act.wait_ge(SC["up_moved"], u - 1)
                    act.activation(sg[0:n, u % 2, 0:w], (bank[0], bank[6])[u % 2][0:n, 0:w], ACT.Silu,
                                   scale=gus[0:n, b:b + 1]).then_inc(SC["silu"], 1)
            for b in range(FB):
                n = FR[b]
                act.wait_ge(SC["h_rounded"], b + 1)
                act.activation(hq[0:n, b, :], hT[0:n, b, :], ACT.Identity, bias=neg_magic[0:n]).then_inc(SC["hq"], 1)


        @block.vector
        def _(dve):
            steps = [0]

            def step(ins):
                steps[0] += 1
                ins.then_inc(S["dve_step"], 1)
                dve.wait_ge(S["dve_step"], steps[0])

            def layernorm(n):
                dve.wait_ge(S["x_in"], 16 * n + 16)
                for h in range(2):
                    dve.bn_stats(stats[:, h, :], x_in[:, h * HALF:(h + 1) * HALF]).then_inc(S["ln_step"], 1)
                dve.drain()
                dve.bn_aggr(mv, stats[:, :, :].rearrange("p a b -> p (a b)")).then_inc(S["ln_step"], 1)
                dve.wait_ge(S["ln_step"], 3 * n + 3)
                dve.tensor_scalar(var_eps, mv[:, 1:2], EPS, None, ALU.add).then_inc(S["var_ready"], 1)
                dve.wait_ge(S["rstd_ready"], n + 1)
                dve.tensor_scalar(x_in, x_in, mv[:, 0:1], rstd, ALU.subtract, ALU.mult).then_inc(S["ln_done"], 1)

            def xT_low(f, par):
                for j in range(2):
                    dve.wait_ge(S["fill_hi"], f + j + 1)
                    s = slice(4 * j, 4 * j + 4)
                    dve.scalar_tensor_tensor(xT[par][:, 1, s, :].rearrange("p k n -> p (k n)"), tp[j][:, :], X_UP,
                                             xT[par][:, 0, s, :].rearrange("p k n -> p (k n)"), ALU.mult,
                                             ALU.subtract).then_inc(S["fill_lo"], 1)

            def qT_low(f):
                for j in range(2):
                    dve.wait_ge(S["fill_hi"], f + j + 1)
                    s = slice(j * HALF, (j + 1) * HALF)
                    dve.tensor_tensor(qT_o[:, 1, s], tp[j][:, :], qT_o[:, 0, s], ALU.subtract).then_inc(S["fill_lo"], 1)

            def weight_low(i):
                for c in range(2):
                    dve.wait_ge(S["w_hi"], 2 * i + 1 + c)
                    s = slice(4 * c, 4 * c + 4)
                    dve.scalar_tensor_tensor(w16[i][:, s, 1, :], w_raw[i][:, s, :], W_UP, w16[i][:, s, 0, :], ALU.mult,
                                             ALU.subtract).then_inc(S["w_lo"], 1)

            def kv_evac(t, j):
                o, b = ((k_t, bk_b), (v_t, bv_b))[j // 2]
                s = slice(j % 2 * HALF, (j % 2 + 1) * HALF)
                if not (isinstance(t, int) and t == 0) and j % 2 == 0:
                    dve.wait_ge(S["kv_done"], t)
                dve.wait_ge(S["unit_full"], UNITS * t + j + 1)
                dve.scalar_tensor_tensor(o[:, s], proj[j % 2][:, :], 1.0 / (X_UP * W_UP), b[:, s], ALU.mult,
                                         ALU.add).then_inc(S["dve_evac"], 1)

            step(dve.memset(cols[:, :], 0.0))
            for c, value in ((neg_magic, -MAGIC), (ones, 1.0), (exponent, -0.5), (half_neg, -0.5)):
                step(dve.memset(c, value))
            step(dve.memset(ones_r[:, :], 1.0))
            step(dve.memset(keyT[:, C:C + CU], -1.0))
            dve.nop().then_inc(SC["c_step"], 1)
            dve.nop().then_inc(SB["a_more_used"], 1)
            layernorm(0)
            xT_low(0, 0)
            weight_low(0)
            weight_low(1)
            dve.wait_ge(S["bias_in"], 48)
            kv_evac(0, 0)
            weight_low(2)
            kv_evac(0, 1)
            weight_low(3)
            dve.wait_ge(S["edges_in"], 64)
            for b, (_, n) in enumerate(EB):
                dst_i, src_i = e_dst[0:n, b, :].bitcast(I32), e_src[0:n, b, :].bitcast(I32)
                step(dve.tensor_reduce(e_min[0:n, b:b + 1], dst_i, AX.X, ALU.min))
                step(dve.tensor_reduce(e_span[0:n, b:b + 1], dst_i, AX.X, ALU.max))
                step(dve.tensor_tensor(e_span[0:n, b:b + 1], e_span[0:n, b:b + 1], e_min[0:n, b:b + 1], ALU.subtract))
                step(dve.tensor_scalar(e_dst[0:n, b, :], dst_i, e_min[0:n, b:b + 1], float(T), ALU.subtract, ALU.mult))
                step(dve.tensor_scalar(e_tmp[0:n].bitcast(I32), src_i, 7, None, ALU.logical_shift_right))
                step(dve.tensor_tensor(e_dst[0:n, b, :], e_dst[0:n, b, :], e_tmp[0:n].bitcast(I32), ALU.add))
                step(dve.tensor_scalar(e_tmp[0:n].bitcast(I32), src_i, P - 1, None, ALU.bitwise_and))
                step(dve.tensor_copy(e_src[0:n, b, :], e_tmp[0:n].bitcast(I32)))
            dve.nop().then_inc(S["edges_ready"], 1)
            kv_evac(0, 2)
            weight_low(4)
            dve.wait_ge(S["edges_T"], 1)
            dve.tensor_scalar(base_row[:, :], tp[0][0:1, 0:C], float(T), None, ALU.mult).then_inc(S["columns"], 1)
            dve.tensor_copy(loT[0:EC, :], agg[1][0:EC, 0:C]).then_inc(S["columns"], 1)
            dve.tensor_copy(keyT[0:EC, 0:C], agg[0][0:EC, 0:C]).then_inc(S["columns"], 1)
            dve.tensor_copy(bq_c[:, :], tp[0][:, C:C + K]).then_inc(S["columns"], 1)
            dve.tensor_reduce(flags[:, 0:1], tp[1][0:1, 0:C], AX.X, ALU.max).then_inc(S["columns"], 1)
            kv_evac(0, 3)
            weight_low(5)
            weight_low(6)
            weight_low(7)
            layernorm(1)
            dve.wait_ge(S["counts_set"], 1)
            dve.wait_ge(S["consts"], 3)
            by_node = counts[:, :].rearrange("p (n s) -> p n s", s=T)
            for t in range(T):
                r = P if t < T - 1 else LAST
                step(dve.tensor_copy(by_node[:, t * P:t * P + r, t], ident[:, 0:r]))
            dve.wait_ge(S["columns"], 5)

            def one_hot_dst(u, i):
                c0, n = GROUPS[i]
                for cc in range(c0, c0 + n):
                    dve.tensor_scalar(hot_dst[0:EC, cc, :], iota_w[0:EC, :], keyT[0:EC, bass.ds(u * CU + cc, 1)],
                                      None, ALU.is_equal).then_inc(S["hot_dst_ready"], 1)

            def count(u, i, first):
                dve.wait_ge(S["adj_mm"], 2 * u + i + 1)
                c0, n = GROUPS[i]
                for cc in range(n):
                    c = u * CU + c0 + cc
                    at = dve.value_load(base_row[0:1, bass.ds(c, 1)], min_val=0, max_val=(N - 1) * T)
                    if not (first and i == 0 and cc == 0):
                        dve.wait_ge(S["adj_added"], c)
                    window = counts[:, bass.ds(at, WC)]
                    dve.tensor_tensor(window, agg[i][:, cc * WC:(cc + 1) * WC], window,
                                      ALU.add).then_inc(S["adj_added"], 1)
                one_hot_dst(u + 1, i)

            one_hot_dst(0, 0)
            one_hot_dst(0, 1)
            xT_low(2, 1)
            qT_low(4)

            def tile(t, par, first):
                for j in range(UNITS):
                    u = UNITS * (t - 1) + j
                    for i in range(2):
                        count(u, i, first and j == 0)
                    if j < 4:
                        kv_evac(t, j)
                    if j == 1:
                        layernorm(t + 1)
                    if j == 3:
                        xT_low(4 * t + 2, 1 - par)
                qT_low(4 * t + 4)

            counted_tiles(dve, tile)

            dve.wait_ge(S["adj_added"], C)
            span = dve.value_load(flags[0:1, 0:1], min_val=0, max_val=N)
            with dve.If(span >= W):
                with dve.Fori(1, WINDOWS) as k:
                    dve.drain()
                    dve.tensor_scalar(keyT[0:EC, :], keyT[0:EC, :], float(-WC), None, ALU.add)
                    dve.tensor_scalar(base_row[:, :], base_row[:, :], float(WC), float(N * T), ALU.add, ALU.min)
                    dve.drain()
                    with dve.Fori(0, C) as c:
                        dve.tensor_scalar(hot_dst[0:EC, 0, :], iota_w[0:EC, :], keyT[0:EC, bass.ds(c, 1)],
                                          None, ALU.is_equal).then_inc(SE["e_hot"], 1)
                        dve.tensor_scalar(hot_src[0:EC, 0, 0, :], iota_p[0:EC, :], loT[0:EC, bass.ds(c, 1)],
                                          None, ALU.is_equal).then_inc(SE["e_hot"], 1)
                        at = dve.value_load(base_row[0:1, bass.ds(c, 1)], min_val=0, max_val=N * T)
                        window = counts[:, bass.ds(at, WC)]
                        dve.wait_ge(SE["e_mm"], (k - 1) * C + c + 1)
                        dve.tensor_tensor(window, agg[0][:, 0:WC], window, ALU.add)
                        dve.drain()

            step(dve.memset(kvs, 0.0))
            NS = NP // 5
            for j in range(4):
                kv_evac(T - 1, j)
                for q in ((0, 1), (2,), (3,), (4,))[j]:
                    piece = by_node[:, q * NS:(q + 1) * NS, :]
                    dve.tensor_reduce(sources[:, q * NS:(q + 1) * NS], piece, AX.X, ALU.add).then_inc(S["dve_step"], 1)
                    dve.tensor_reduce(most_c[:, q:q + 1], piece, AX.XY, ALU.max).then_inc(S["dve_step"], 1)
                    steps[0] += 2
            dve.wait_ge(S["dve_step"], steps[0])
            dve.nop().then_inc(SM["sources"], 1)
            step(dve.tensor_reduce(m_col, most_c, AX.X, ALU.max))
            dve.nop().then_inc(SM["max_col"], 1)
            dve.wait_ge(S["kv_done"], T)
            for b in range(2):
                acc = kv_acc[b][:, :].rearrange("p (q n) -> p q n", n=P)
                for h in range(2):
                    r = slice(h * DH, (h + 1) * DH)
                    dve.tensor_scalar(kvs[r, 4 * b:4 * b + 4, r], acc[r, :, r], M_UP / (N * DH), None,
                                      ALU.mult).then_inc(SM["kvs"], 1)
            dve.wait_ge(SM["deg_full"], 1)
            dve.tensor_scalar(dinv, agg[0][:, 0:T], 1.0, None, ALU.max).then_inc(SM["deg_ready"], 1)
            dve.wait_ge(SM["max_T"], 1)
            dve.tensor_reduce(flags[:, 1:2], agg[1][0:1, 0:P], AX.X, ALU.max).then_inc(SM["max_col"], 1)

            def counts_tile(t):
                return counts[:, bass.ds(t * P * T, P * T)].rearrange("p (n s) -> p s n", s=T)

            def a_tile(t):
                dve.tensor_scalar(a_t, counts_tile(t), float(COUNT_MAX), None, ALU.min).then_inc(SB["a_ready"], 1)

            a_tile(0)
            qT_low(4 * T - 2)
            for i in range(2 * PAIRS):
                dve.wait_ge(SM["m_hi"], i + 1)
                s = slice((i % 2) * HALF, (i % 2 + 1) * HALF)
                dve.tensor_tensor(m16[1][:, i // 2, s], proj[i % 2][:, :], m16[0][:, i // 2, s],
                                  ALU.subtract).then_inc(SM["m_lo"], 1)
            dve.wait_ge(SM["dinv"], 3)
            for t in range(T):
                dve.wait_ge(SM["h_hi"], t + 1)
                dve.scalar_tensor_tensor(h16[:, t, D:2 * D], g_in[t % 2], dinv_up[:, t:t + 1], h16[:, t, 0:D], ALU.mult,
                                         ALU.subtract).then_inc(SM["h_lo"], 1)
            step(dve.memset(ones_m, 1.0))
            dve.wait_ge(SM["b_bias_in"], 32)
            dve.wait_ge(SM["max_col"], 2)
            most = dve.value_load(flags[0:1, 1:2], min_val=0, max_val=E + 1)

            def weight_scale(i, w, n):
                step(dve.tensor_reduce(wsc[0:n, i:i + 1], w, AX.X, ALU.max, apply_absolute_value=True))
                step(dve.tensor_scalar(wsc[0:n, i:i + 1], wsc[0:n, i:i + 1], 1.0 / QMAX, None, ALU.mult))
                step(dve.reciprocal(wrc[0:n, i:i + 1], wsc[0:n, i:i + 1]))
                step(dve.tensor_scalar(w, w, wrc[0:n, i:i + 1], MAGIC, ALU.mult, ALU.add))
                step(dve.tensor_scalar(w, w, MAGIC + QMAX, MAGIC - QMAX - 1.0, ALU.min, ALU.max))

            def piece(i):
                kind, a, b = pieces[i]
                dve.wait_ge(SF[f"raw_in{i % 2}"], 16 * (i // 2 + 1))
                if kind == "gu":
                    weight_scale(FB * a + b, raw[i % 2][0:FR[b], :], FR[b])
                else:
                    for k in range(2):
                        kk = a + k
                        weight_scale(2 * FB + kk, raw[i % 2][:, k * FF:(k + 1) * FF], P)
                        if kk >= 2:
                            dve.wait_ge(SF["drow_full"], kk - 1)
                        dve.tensor_scalar(diag[:, kk % 2, :], ident[:, :], wsc[:, 2 * FB + kk:2 * FB + kk + 1], None,
                                          ALU.mult).then_inc(SF["diag"], 1)
                dve.nop().then_inc(SF["wq_ready"], 1)

            def tile_b(t, par, t2):
                fixed = isinstance(t, int)
                last_tile = fixed and t == T - 1
                row_x2 = x2[:, bass.ds(t, 1), :].rearrange("p a d -> p (a d)")

                def beside(product):
                    if fixed and (t, product) in slots:
                        piece(slots.index((t, product)))

                dve.wait_ge(SB["x_bias"], t + 1)
                for n in range(2):
                    s = slice(n * HALF, (n + 1) * HALF)
                    beside(n)
                    dve.wait_ge(SB["mix_full"], 2 * t + n + 1)
                    dve.scalar_tensor_tensor(row_x2[:, s], proj[n][:, :], 1.0 / M_UP, x_t[par][:, s], ALU.mult,
                                             ALU.add).then_inc(SB["mix_moved"], 1)
                beside(2)
                beside(3)
                with dve.If(most > COUNT_MAX):
                    with dve.Fori(0, ROUNDS - 1) as r:
                        dve.wait_ge(SB["agg_full"], 2 * t + 2)
                        dve.wait_ge(SB["a_more_used"], t * (ROUNDS - 1) + r + 1)
                        dve.tensor_scalar(counts_tile(t), counts_tile(t), float(-COUNT_MAX), 0.0, ALU.add, ALU.max)
                        dve.drain()
                        dve.tensor_scalar(a_t, counts_tile(t), float(COUNT_MAX), None, ALU.min).then_inc(SB["a_more"], 1)
                    dve.wait_ge(SB["a_more_used"], (t + 1) * (ROUNDS - 1) + 1)
                    dve.memset(stats[:, 0, 0:1], 0.0)
                for n in range(2):
                    s = slice(n * HALF, (n + 1) * HALF)
                    dve.wait_ge(SB["agg_full"], 2 * t + n + 1)
                    dve.scalar_tensor_tensor(agg[n][:, :], agg[n][:, :], dinv_down[:, bass.ds(t, 1)], gb_b[:, s],
                                             ALU.mult, ALU.add)
                    dve.drain()
                    dve.scalar_tensor_tensor(row_x2[:, s], agg[n][:, :], 0.0, row_x2[:, s], ALU.max,
                                             ALU.add).then_inc(SB["agg_moved"], 1)
                    dve.drain()
                    dve.bn_stats(stats[:, n, :], row_x2[:, s])
                if not last_tile:
                    a_tile(t + 1)
                dve.drain()
                dve.bn_aggr(mv, stats[:, :, :].rearrange("p a b -> p (a b)"))
                dve.drain()
                dve.tensor_scalar(var_eps, mv[:, 1:2], EPS, None, ALU.add).then_inc(SB["b_var"], 1)
                dve.wait_ge(SB["b_rstd"], t + 1)
                dve.tensor_scalar(x_t[par], row_x2, mv[:, 0:1], rstd, ALU.subtract, ALU.mult).then_inc(SB["b_norm"], 1)
                dve.tensor_copy(ln_mean[:, bass.ds(t, 1)], mv[:, 0:1])
                dve.tensor_copy(ln_rstd[:, bass.ds(t, 1)], rstd)
                dve.drain()
                r = LAST if last_tile else P
                dve.tensor_reduce(mx[0:r, bass.ds(t, 1)], x_t[par][0:r, :], AX.X, ALU.max,
                                  apply_absolute_value=True).then_inc(SB["b_max"], 1)

            over_tiles(dve, tile_b)

            dve.wait_ge(SF["drow_full"], K)
            for j in range(2):
                step(dve.tensor_copy(d_row[:, j * HALF:(j + 1) * HALF], kv_acc[j][:, :]))

            def scale(i, columns, dst, rdst):
                step(dve.tensor_reduce(m_col, columns, AX.X, ALU.max))
                dve.nop().then_inc(SC["m_ready"], 1)
                if i == 0:
                    dve.wait_ge(SC["exp"], 1)
                step(dve.tensor_scalar(row[:, 4:5], row[:, 2 + i:3 + i], 1.0, None, ALU.add))
                step(dve.reciprocal(row[:, 5:6], row[:, 4:5]))
                dve.wait_ge(SC["m_T"], i + 1)
                step(dve.tensor_reduce(row[:, 7:8], bank[2][0:1, 0:P], AX.X, ALU.max))
                step(dve.tensor_tensor(row[:, 7:8], row[:, 7:8], row[:, 5:6], ALU.mult))
                dve.tensor_scalar(row[:, 6:7], row[:, 7:8], 1.0 / QMAX, None, ALU.mult).then_inc(SC["s_row"], 1)
                dve.wait_ge(SC["s_bc"], i + 1)
                step(dve.tensor_copy(dst, bank[3][:, 0:1]))
                step(dve.reciprocal(rdst, dst))

            dve.wait_ge(SB["b_max"], T)
            scale(0, mx, s_x, rs_x)
            step(dve.tensor_scalar(gus, wsc[:, 0:2 * FB], s_x, None, ALU.mult))

            def xq_tile(t):
                if t >= 2:
                    dve.wait_ge(SC["qT_full"], 2 * t - 2)
                q = q_c[t % 2]
                step(dve.tensor_scalar(q, x2[:, t, :], ln_mean[:, t:t + 1], ln_rstd[:, t:t + 1], ALU.subtract, ALU.mult))
                step(dve.tensor_scalar(q, q, rs_x, MAGIC, ALU.mult, ALU.add))
                dve.tensor_scalar(q, q, MAGIC + QMAX, MAGIC - QMAX - 1.0, ALU.min, ALU.max).then_inc(SC["q_ready"], 1)

            for what, c in FFN_ORDER:
                if what == "quantise":
                    for t in TILES_OF[c]:
                        xq_tile(t)
                    continue
                c0, w = NCH[c]
                for b in range(FB):
                    u, n = FB * c + b, FR[b]
                    dve.wait_ge(SC["gate_full"], 2 * u + 2)
                    dve.wait_ge(SC["silu"], u + 1)
                    dve.scalar_tensor_tensor(hT[0:n, b, c0:c0 + w], (bank[1], bank[7])[u % 2][0:n, 0:w],
                                             gus[0:n, FB + b:FB + b + 1], sg[0:n, u % 2, 0:w], ALU.mult,
                                             ALU.mult).then_inc(SC["up_moved"], 1)
                    dve.wait_ge(SC["up_moved"], u + 1)
                    step(dve.tensor_reduce(mh[0:n, u:u + 1], hT[0:n, b, c0:min(c0 + w, N)], AX.X, ALU.max,
                                           apply_absolute_value=True))
            scale(1, mh, s_d, rs_d)
            for b in range(FB):
                a = hT[0:FR[b], b, :]
                step(dve.tensor_scalar(a, a, rs_d[0:FR[b]], MAGIC, ALU.mult, ALU.add))
                dve.tensor_scalar(a, a, MAGIC + QMAX, MAGIC - QMAX - 1.0, ALU.min, ALU.max).then_inc(SC["h_rounded"], 1)

            with dve.Fori(0, T // 2) as t2:
                for par in range(2):
                    t = 2 * t2 + par
                    row_x2 = x2[:, bass.ds(t, 1), :].rearrange("p a d -> p (a d)")
                    for n in range(2):
                        s = slice(n * HALF, (n + 1) * HALF)
                        dve.wait_ge(SC["y_full"], 2 * t + n + 1)
                        dve.scalar_tensor_tensor(y_t[:, s], (bank[0:2], bank[6:8])[par][n][:, :], s_d, d_row[:, s],
                                                 ALU.mult, ALU.mult).then_inc(SC["y_moved"], 1)
                        dve.wait_ge(SC["y_moved"], 2 * t + n + 1)
                        dve.tensor_tensor(row_x2[:, s], row_x2[:, s], y_t[:, s], ALU.add).then_inc(SC["y_ready"], 1)

_INS = ['x', 'src', 'dst', 'L0_gnn_W', 'L0_gnn_b', 'L0_mix_Wq', 'L0_mix_bq', 'L0_mix_Wk', 'L0_mix_bk', 'L0_mix_Wv',
        'L0_mix_bv', 'L0_mix_Wo', 'L0_mix_bo', 'L0_ffn_clip_x', 'L0_ffn_clip_down', 'L0_ffn_w_gate', 'L0_ffn_w_up',
        'L0_ffn_w_down']


def kernel(**inputs):
    import numpy as np
    import concourse.bacc as bacc
    from concourse.bass_utils import run_bass_kernel_spmd

    nc = bacc.Bacc("TRN2", target_bir_lowering=False, num_devices=1)
    arrays, args = {}, []
    for name in _INS:
        a = np.ascontiguousarray(inputs[name])
        arrays[f"in_{name}"] = a
        args.append(nc.dram_tensor(f"in_{name}", a.shape, mybir.dt.from_np(a.dtype), kind="ExternalInput").ap())
    out = nc.dram_tensor("out_x", (N, D), F32, kind="ExternalOutput").ap()
    gps_layer(nc, *args, out)
    r = run_bass_kernel_spmd(nc, [arrays], core_ids=[0])
    return r.results[0]["out_x"]
```

```python
from contextlib import ExitStack

import concourse.bass as bass
from concourse import mybir

ALU = mybir.AluOpType
ACT = mybir.ActivationFunctionType
AX = mybir.AxisListType
F32 = mybir.dt.float32
F16 = mybir.dt.float16
BF16 = mybir.dt.bfloat16
I32 = mybir.dt.int32
U32 = mybir.dt.uint32
U16 = mybir.dt.uint16

P = 128
HALF = 512
N, D = 1250, 1024
T = -(-N // P)
LAST = N - (T - 1) * P
NP = T * P
K = D // P
HEADS, DH = 16, 64
PAIRS = HEADS // 2
E = 40000
EC = 125
C = E // EC
W = 16
WC = W * T
WINDOWS = -(-N // W)
G = 3
KV_GROUPS, LATE_GROUPS, Q_GROUPS = 4, 5, (16, 12)
GROUPS = T * KV_GROUPS + (T - 2) * LATE_GROUPS + sum(Q_GROUPS)
CP = GROUPS * G
FF = 352
FB = -(-FF // P)
FR = [min(P, FF - P * b) for b in range(FB)]
QMAX = 127.0
MAGIC = 1.5 * 2.0 ** 23
EPS = 1e-5
EB = [(0, P), (P, P), (2 * P, C - 2 * P)]
NCH = [(0, 512), (512, 512), (1024, 256)]
QCH = [(0, 4), (4, 3), (7, 3)]
X_UP = W_UP = 2.0 ** 8
M_UP, H_UP = 2.0 ** 8, 2.0 ** 4
COUNT_MAX = 2048
ROUNDS = -(-(E + 1) // COUNT_MAX)
assert E == EC * C and CP >= C and T == 10


def gps_layer(nc, x, src, dst, gnn_W, gnn_b, Wq, bq, Wk, bk, Wv, bv, Wo, bo,
              clip_x, clip_down, w_gate, w_up, w_down, out):
    with ExitStack() as ctx:
        def sb(name, shape, dt):
            return ctx.enter_context(nc.sbuf_tensor(name, shape, dt))

        def sems(*names):
            return {n: ctx.enter_context(nc.semaphore(n)) for n in names}

        bank = [ctx.enter_context(nc.psum_tensor(f"bank{i}", [P, HALF], F32)) for i in range(8)]
        proj, kv_acc, tp, agg = bank[0:2], bank[2:4], bank[4:6], bank[6:8]
        m_bank = tp + proj

        SLOT = K * HALF
        mem = sb("mem", [P, 8 * SLOT + 11 * D], F32)

        def part(at, *dims, dt=F32):
            size = 1
            for d in dims:
                size *= d
            words = size * (2 if dt in (F16, BF16) else 4) // 4
            a = mem[:, at:at + words]
            if dt != F32:
                a = a.bitcast(dt)
            if len(dims) == 2:
                a = a.rearrange("p (a b) -> p a b", b=dims[1])
            if len(dims) == 3:
                a = a.rearrange("p (a b c) -> p a b c", b=dims[1], c=dims[2])
            return a

        slot_at = [2 * SLOT, 3 * SLOT, 0, SLOT]
        w16 = [part(slot_at[i % 4], K, 2, HALF, dt=F16) for i in range(8)]
        XIN = 4 * SLOT
        x_in = [part(XIN + i * D, D) for i in range(2)]
        RAW = XIN + 2 * D
        w_raw = [part(0 if i == 1 else RAW, K, HALF) for i in range(8)]
        QT = RAW + SLOT
        qT = part(QT, T, 2 * K, P, dt=F16)
        k_t, v_t = [[part(QT + (2 * j + i) * HALF, HALF) for i in range(2)] for j in range(2)]
        bk_b, bv_b = [part(QT + 2 * D + i * D, D) for i in range(2)]
        e_src, e_dst = [part(QT + 4 * D + 3 * EC * i, 3, EC) for i in range(2)]
        e_tmp = part(QT + 4 * D + 6 * EC, 3, EC)
        bq_rows = part(QT + 6 * D, P)[0:K]
        XT = QT + T * D
        xT = part(XT, 2 * K, NP, dt=F16)
        kvs = part(XT + T * D, PAIRS, P)
        assert XT + T * D + D == 8 * SLOT + 11 * D
        sources = part(RAW, NP)
        w16_q = part(2 * SLOT, 4 * K, HALF, dt=F16)
        h16 = part(2 * SLOT, T, 2 * D, dt=F16)
        wo = [part(RAW, K, HALF), part(0, K, HALF)]
        m16 = [part(XT + i * SLOT, K, D, dt=F16) for i in range(2)]
        x2 = part(QT - D, T, D)
        gb_b, *x_t = [part(RAW + i * D, D) for i in range(3)]
        bo_b = part(XT + T * D, D)
        a_t = [part(XT + 2 * SLOT + i * T * P // 2, T, P, dt=F16) for i in range(2)]
        raw = [part(i * D, D) for i in range(2)]
        at = 2 * D
        wguT = part(at, K * 2, FF, dt=BF16)
        at += K * FF
        wdT = part(at, FB, D, dt=BF16)
        at += FB * D // 2
        d_row = part(at, D)
        at += D
        ones_m = part(at, P)
        diag = part(at + P, 4, P)
        assert at + 5 * P <= 2 * SLOT
        C0 = XT
        H0 = 2 * SLOT
        xqT = part(C0, K, NP, dt=BF16)
        C0 += K * NP // 2
        sg = part(C0, 2, HALF)
        q_c = [part(C0 + D + i * D, D) for i in range(2)]
        q16 = [part(C0 + 3 * D + i * D // 2, D, dt=BF16) for i in range(2)]
        assert C0 + 4 * D <= XT + T * D
        hT = part(H0, FB, NP)
        hq = part(H0 + FB * NP, FB, NP, dt=BF16)
        y_t = [part(H0 + FB * NP * 3 // 2 + i * D, D) for i in range(2)]
        assert FB * NP * 3 // 2 + 2 * D <= T * D

        counts = sb("counts", [P, NP * T], U16)
        keyT = sb("keyT", [P, CP + 2 * G], F32)
        loT = sb("loT", [P, CP + 2 * G], F32)
        base_row = sb("base_row", [1, CP], I32)
        iota_w = sb("iota_w", [P, G, WC], BF16)
        iota_p = sb("iota_p", [P, P], BF16)
        hot_dst_mem = sb("hot_dst", [P, D], BF16)
        hot_dst = hot_dst_mem[:, 0:2 * G * WC].rearrange("p (i g w) -> p i g w", i=2, g=G)
        raw16 = [part(XT + 2 * SLOT + T * P, D, dt=BF16), hot_dst_mem[:, :]]
        hot_src = sb("hot_src", [P, 2, G, P], BF16)
        src_col = sb("src_col", [P, 2, G], F32)
        ident = sb("ident", [P, P], F32)
        ident16 = sb("ident16", [P, P], BF16)
        stats = sb("stats", [P, 2, 6], F32)
        cols = sb("cols", [P, 192], F32)
        col_at = [0]

        def col(n=1):
            col_at[0] += n
            return cols[:, col_at[0] - n:col_at[0]]

        mv, var_eps, exponent, rstd = col(2), col(), col(), col()
        half_neg, dinv, dinv_up, dinv_down = col(T), col(T), col(T), col(T)
        ln_mean, ln_rstd, mx, m_col, ones, neg_magic = col(T), col(T), col(T), col(), col(), col()
        s_x, rs_x, s_d, rs_d = col(), col(), col(), col()
        xn_scale, xn_shift, x_top, x_low, x_ends = col(T), col(T), col(2), col(2), col(2)
        e_min, e_span = col(4), col(4)
        wsc, wrc, gus, mh = col(2 * FB + K), col(2 * FB + K), col(2 * FB), col(9)
        bq_c = sb("bq_c", [P, K], F32)
        row = sb("row", [1, 8], F32)
        flags = sb("flags", [1, 2], I32)
        ones_r = sb("ones_r", [1, P], F32)

        S = sems("consts", "pool_step", "edges_in", "bias_in", "x_in0", "x_in1", "dve_step",
                 *[f"w_in{i}_{c}" for i in range(8) for c in range(2)], "ln_step", "var_ready", "rstd_ready", "edges_ready",
                 "edges_T", "columns", "scratch_set", "ln_done", "xT_full", "xT_hi", "xT_lo", "w_hi", "w_lo", "kv_full", "kv_evac",
                 "k_relu", "kv_done", "q_full", "q_relu", "q_hi", "q_lo", "g_full", "h_hi", "h_lo", "hot_dst_ready",
                 "hot_src_ready", "adj_mm", "adj_added", "counts_set")
        SE = sems("e_hot", "e_mm")
        SM = sems("wo_in0", "wo_in1", "gb_in", "bo_in", "kvs", "sources", "deg_full", "deg_ready", "dinv", "prod_full",
                  "m_hi", "m_lo", "max_col", "max_T")
        SB = sems("xb_in0", "xb_in1", "x_bias", "a_ready", "mix_full", "agg_full", "mix_moved", "agg_moved",
                  "b_var", "b_rstd", "b_max", "a_more", "a_more_used")
        SF = sems("raw_in0", "raw_in1", "wq_ready", "w16_ready", "wT_full", "wT_moved", "diag", "drow_full")
        SC = sems("clip_in", "c_step", "m_ready", "m_T", "s_row", "s_bc", "exp", "xn_columns", "affine", "q_ready", "qT_full",
                  "qT_moved", "gate_full", "silu", "up_moved", "h_rounded", "hq", "y_full", "y_moved", "y_ready0", "y_ready1", "stored")

        def over_tiles(eng, tile):
            tile(0, 0, 0)
            tile(1, 1, 0)
            with eng.Fori(1, T // 2 - 1) as t2:
                for par in range(2):
                    tile(2 * t2 + par, par, t2)
            tile(T - 2, 0, T // 2 - 1)
            tile(T - 1, 1, T // 2 - 1)

        def kv_tiles(eng, tile):
            for t in (2, 3):
                tile(0, t, t % 2, t // 2)
            with eng.Fori(2, T // 2 - 1) as t2:
                for par in range(2):
                    tile(0, 2 * t2 + par, par, t2)
            for t in (T - 2, T - 1):
                tile(0, t, t % 2, t // 2)
            for t in (0, 1):
                tile(1, t, t, 0)
            with eng.Fori(1, T // 2) as t2:
                for par in range(2):
                    tile(1, 2 * t2 + par, par, t2)

        GROUP_AT = {0: (), 2: (10, 22), 3: (4, 14, 24), 4: (6, 12, 18, 24)}

        def kv_halves(h, t, groups):
            half = 0 if isinstance(t, int) and (h, t) == (0, 2) else len(groups) // 2
            return groups[:half], groups[half:]

        def kv_groups(h, t, par):
            n, first = KV_GROUPS, (T * h + t - 2) * KV_GROUPS
            if h == 1 and not isinstance(t, int):
                n, first = LATE_GROUPS, T * KV_GROUPS + (t - 2) * LATE_GROUPS
            return [(first + i, (n * par + i) % 2) for i in range(n)]

        def q_groups(c, q, j):
            n = Q_GROUPS[c] // 8
            extra = Q_GROUPS[c] % 8 // 4
            first = T * KV_GROUPS + (T - 2) * LATE_GROUPS + sum(Q_GROUPS[:c]) + q * (Q_GROUPS[c] // 2)
            at = j * n + j // 2 * extra
            return [(first + at + i, (at + i) % 2) for i in range(n + extra * (j % 2))]

        pieces = [("gu", m, b) for m in range(2) for b in range(FB)] + [("down", k, 0) for k in range(0, K, 2)]
        slots = [(0, 2), (0, 3), (1, 0), (1, 2), (1, 3), (T - 2, 0), (T - 2, 2), (T - 2, 3), (T - 1, 1), (T - 1, 2)]
        pe_slots = [(0, 3), (1, 0), (1, 1), (1, 3), (T - 2, 0), (T - 2, 1), (T - 2, 3), (T - 1, 0), (T - 1, 2), (T - 1, 3)]
        moves_of = [1 if kind == "gu" else 2 for kind, _, _ in pieces]

        UNIT = [(c, b) for c in range(len(NCH)) for b in range(FB)]
        HQ_PARTS = [(c0, w, b0, nb) for c0, w in ((0, P), (P, 3 * P), (4 * P, 4 * P), (8 * P, 2 * P))
                    for b0, nb in ((0, FB - 1), (FB - 1, 1))]
        WEIGHTS_AFTER = {(1, K - 1): ((6, 0), (6, 1)), (2, 1): ((7, 0),), (2, 2): ((7, 1),)}
        LOWS_AFTER = {(1, K - 1): ((6, 0),), (2, 0): ((6, 1),), (2, 1): ((7, 0),), (2, 2): ((7, 1),)}
        Q = [("q", t) for t in range(T)]
        U = [("u", u) for u in range(len(UNIT))]
        PE_FFN = Q[:4] + U[:2] + Q[4:8] + U[2:5] + Q[8:] + U[5:]
        ACT_FFN = Q[:4] + U[:2] + Q[4:8] + U[2:5] + Q[8:] + U[5:]
        DVE_FFN = Q[:8] + U[:3] + Q[8:] + U[3:]
        AFFINE_AFTER = {0: 3, 2: 5, 3: 7, 7: 9}

        def weights_beside(h, t):
            return {(0, T - 2): 2, (0, T - 1): 3, (1, 0): 4, (1, 1): 5}.get((h, t)) if isinstance(t, int) else None

        block = ctx.enter_context(nc.Block())


        @block.sync
        def _(sp):
            halves = [(w, h) for h, ws in ((0, (Wk, Wv)), (1, (Wk, Wv)), (0, (Wq,)), (1, (Wq,)), (0, (gnn_W,)), (1, (gnn_W,)))
                      for w in ws]

            def load_w(i):
                w, h = halves[i]
                for c in range(2):
                    if i >= 2:
                        sp.wait_ge(S["w_lo"], c + 1 if i == 2 else 2 * i - 1 + c)
                    sp.dma_start(w_raw[i][:, 4 * c:4 * c + 4, :],
                                 w.rearrange("(k p) n -> p k n", p=P)[:, 4 * c:4 * c + 4, h * HALF:(h + 1) * HALF]
                                 ).then_inc(S[f"w_in{i}_{c}"], 16)

            def load_x(t, rows=P):
                if t >= 2:
                    sp.wait_ge(S["xT_full"], 2 * t - 2)
                sp.dma_start(x_in[t % 2][0:rows, :], x[t * P:t * P + rows, :]).then_inc(S[f"x_in{t % 2}"], 16)

            load_x(0)
            load_w(0)
            load_x(1)
            sp.wait_ge(S["scratch_set"], 2)
            for e, a in ((e_dst.bitcast(I32), dst), (e_src.bitcast(I32), src)):
                ev = a.rearrange("(c e) -> c e", e=EC)
                sp.dma_start(e[:, 0:2, 0:EC], ev[0:2 * P].rearrange("(b p) e -> p b e", p=P)).then_inc(S["edges_in"], 16)
                sp.dma_start(e[0:EB[2][1], 2, 0:EC], ev[2 * P:C]).then_inc(S["edges_in"], 16)
            load_w(1)
            for b_sb, b in ((bk_b, bk), (bv_b, bv)):
                sp.dma_start(b_sb, b.rearrange("(a n) -> a n", a=1).broadcast_to([P, D])).then_inc(S["bias_in"], 16)
            sp.dma_start(bq_rows, bq.rearrange("(k p) -> k p", p=P)).then_inc(S["bias_in"], 16)
            for i, clip in enumerate((clip_x, clip_down)):
                sp.dma_start(row[:, i:i + 1], clip.rearrange("(a n) -> a n", a=1)).then_inc(SC["clip_in"], 16)
            load_x(2)
            load_w(2)
            load_x(3)
            for t in range(4, T):
                load_x(t, LAST if t == T - 1 else P)
            load_w(3)
            load_w(4)
            for i in (5, 6, 7):
                load_w(i)

            def load_wo(n):
                sp.dma_start(wo[n], Wo.rearrange("(k p) n -> p k n", p=P)[:, :, n * HALF:(n + 1) * HALF]).then_inc(SM[f"wo_in{n}"], 16)

            sp.wait_ge(SM["deg_full"], 1)
            sp.wait_ge(SM["max_col"], 1)
            load_wo(0)
            sp.wait_ge(S["g_full"], T)
            load_wo(1)
            sp.wait_ge(SM["prod_full"], PAIRS)
            sp.dma_start(gb_b, gnn_b.rearrange("(a n) -> a n", a=1).broadcast_to([P, D])).then_inc(SM["gb_in"], 16)
            sp.dma_start(x_t[0], x[0:P, :]).then_inc(SB["xb_in0"], 16)
            sp.dma_start(x_t[1], x[P:2 * P, :]).then_inc(SB["xb_in1"], 16)
            sp.wait_ge(SM["prod_full"], 2 * PAIRS)
            sp.dma_start(bo_b, bo.rearrange("(a n) -> a n", a=1).broadcast_to([P, D])).then_inc(SM["bo_in"], 16)

            def load_piece(i):
                kind, a, b = pieces[i]
                if i < 2:
                    sp.wait_ge(SM["prod_full"], 2 * PAIRS)
                else:
                    sp.wait_ge(SF["w16_ready"], i - 1)
                if kind == "gu":
                    sp.dma_start(raw[i % 2][0:FR[b], :], (w_gate, w_up)[a][b * P:b * P + FR[b], :]).then_inc(SF[f"raw_in{i % 2}"], 16)
                else:
                    sp.dma_start(raw[i % 2][:, 0:2 * FF].rearrange("p (k i) -> p k i", i=FF),
                                 w_down[a * P:(a + 2) * P, :].rearrange("(k p) i -> p k i", p=P)).then_inc(SF[f"raw_in{i % 2}"], 16)

            LOADS = {0: range(2, 4), 1: range(4, 7), T - 2: range(7, 10)}
            load_piece(0)
            load_piece(1)

            def tile(t, par, t2):
                fixed = isinstance(t, int)
                if fixed and t in LOADS:
                    for i in LOADS[t]:
                        load_piece(i)
                if not (fixed and t >= T - 2):
                    sp.wait_ge(SB["b_max"], t + 1)
                    rows = LAST if fixed and t == T - 3 else P
                    sp.dma_start(x_t[par][0:rows, :], x[bass.ds(P * t + 2 * P, rows), :]).then_inc(SB[f"xb_in{par}"], 16)

            tile(0, 0, 0)
            tile(1, 1, 0)
            with sp.Fori(1, T // 2 - 2) as t2:
                for par in range(2):
                    tile(2 * t2 + par, par, t2)
            for t in range(T - 4, T):
                tile(t, t % 2, t // 2)

            def store_out(t, rows):
                for n in range(2):
                    sp.wait_ge(SC[f"y_ready{n}"], t + 1)
                sp.dma_start(out[bass.ds(P * t, rows), :],
                             x2[0:rows, bass.ds(t, 1), :].rearrange("p a d -> p (a d)")).then_inc(SC["stored"], 16)
            with sp.Fori(0, T - 1) as t:
                store_out(t, P)
            store_out(T - 1, LAST)
            sp.wait_ge(SC["stored"], 16 * T)


        @block.gpsimd
        def _(pool):
            pool.memset(ident[:, :], 0.0).then_inc(S["pool_step"], 1)
            pool.memset(counts[:, :].bitcast(U32), 0).then_inc(S["counts_set"], 1)
            pool.wait_ge(S["pool_step"], 1)
            pool.affine_select(out=ident[:, :], in_=ident[:, :], compare_op=ALU.not_equal, fill=1.0, base=0,
                               pattern=[[-1, P]], channel_multiplier=1).then_inc(S["consts"], 1)
            pool.iota(iota_w[:, :, :], [[0, G], [1, WC]], base=0, channel_multiplier=0,
                      allow_small_or_imprecise_dtypes=True).then_inc(S["consts"], 1)
            pool.iota(iota_p[:, :], [[1, P]], base=0, channel_multiplier=0,
                      allow_small_or_imprecise_dtypes=True).then_inc(S["consts"], 1)

            def inverse_deviation(n):
                pool.wait_ge(S["var_ready"], n + 1)
                pool.tensor_tensor(rstd, var_eps, exponent, ALU.pow).then_inc(S["rstd_ready"], 1)

            for n in range(4):
                inverse_deviation(n)

            def one_hot_src(g, i):
                pool.tensor_copy(src_col[0:EC, i, :], loT[0:EC, bass.ds(g * G, G)])
                pool.drain()
                for c in range(G):
                    pool.tensor_scalar(hot_src[0:EC, i, c, :], iota_p[0:EC, :], src_col[0:EC, i, c:c + 1], None,
                                       ALU.is_equal).then_inc(S["hot_src_ready"], 1)

            def after_group(g, i):
                pool.wait_ge(S["adj_mm"], g + 1)
                pool.wait_ge(S["consts"], 3)
                one_hot_src(g + 2, i)

            pool.wait_ge(S["columns"], 2)
            pool.wait_ge(S["consts"], 3)
            one_hot_src(0, 0)
            one_hot_src(1, 1)

            def tile(h, t, par, t2):
                if h == 0 and not (isinstance(t, int) and t >= T - 2):
                    inverse_deviation(t + 2)
                for g, i in kv_groups(h, t, par):
                    after_group(g, i)

            kv_tiles(pool, tile)
            for c in range(2):
                with pool.Fori(0, 2) as q:
                    for j in range(4):
                        for g, i in q_groups(c, q, j):
                            after_group(g, i)

            pool.wait_ge(SM["deg_ready"], 1)
            pool.tensor_tensor(dinv, dinv, half_neg, ALU.pow).then_inc(SM["dinv"], 1)
            pool.wait_ge(SM["dinv"], 1)
            pool.tensor_scalar(dinv_up, dinv, H_UP / (X_UP * W_UP), None, ALU.mult).then_inc(SM["dinv"], 1)
            pool.tensor_scalar(dinv_down, dinv, 1.0 / H_UP, None, ALU.mult).then_inc(SM["dinv"], 1)

            pool.wait_ge(SM["bo_in"], 16)

            def tile_b(t, par, t2):
                pool.wait_ge(SB[f"xb_in{par}"], 16 * t2 + 16)
                pool.tensor_tensor(x_t[par], x_t[par], bo_b, ALU.add).then_inc(SB["x_bias"], 1)
                pool.wait_ge(SB["b_var"], t + 1)
                pool.tensor_tensor(rstd, var_eps, exponent, ALU.pow).then_inc(SB["b_rstd"], 1)

            over_tiles(pool, tile_b)

            with pool.Fori(0, T // 2) as t2:
                for par in range(2):
                    t = 2 * t2 + par
                    row_x2 = x2[:, bass.ds(t, 1), HALF:D].rearrange("p a d -> p (a d)")
                    pool.wait_ge(SC["y_moved"], 2 * t + 2)
                    pool.wait_ge(S["consts"], 3)
                    pool.tensor_tensor(row_x2, row_x2, y_t[par][:, HALF:D], ALU.add).then_inc(SC["y_ready1"], 1)


        @block.tensor
        def _(pe):
            def transposes(t, par):
                pe.wait_ge(S["ln_done"], t + 1)
                for j in range(2):
                    if not (isinstance(t, int) and t == 0):
                        pe.wait_ge(S["xT_lo"], 2 * t + j - 1)
                        pe.wait_ge(S["xT_hi"], 2 * t + j - 1)
                    for k in range(4):
                        last = pe.transpose(tp[j][:, k * P:(k + 1) * P],
                                            x_in[par][:, (4 * j + k) * P:(4 * j + k + 1) * P], ident[:, :])
                    last.then_inc(S["xT_full"], 1)

            def count_group(g, i):
                pe.wait_ge(S["hot_src_ready"], G * (g + 1))
                pe.wait_ge(S["hot_dst_ready"], g + 1)
                if not (isinstance(g, int) and g < 2):
                    pe.wait_ge(S["adj_added"], G * (g - 1))
                for c in range(G):
                    last = pe.matmul(agg[i][:, c * WC:(c + 1) * WC], hot_src[0:EC, i, c, :], hot_dst[0:EC, i, c, :],
                                     start=(c == 0), stop=True, skip_group_check=True)
                last.then_inc(S["adj_mm"], 1)

            def node_unit(i, t, o, signal, groups=(), fresh_x=False, fresh_w=False):
                parts = [(k, a, b) for k in range(K) for a, b in ((0, 0), (0, 1), (1, 0))]
                if fresh_x or fresh_w:
                    parts = [(k, a, b) for a, b in ((0, 0), (1, 0), (0, 1)) for k in range(K)]
                for at, (k, a, b) in enumerate(parts):
                    if fresh_x and (a, k) in ((0, 0), (0, 4), (1, 0), (1, 4)) and b == 0:
                        pe.wait_ge(S[("xT_hi", "xT_lo")[a]], 2 * t + k // 4 + 1)
                    if fresh_w and k in (0, 4) and a == 0:
                        pe.wait_ge(S[("w_hi", "w_lo")[b]], 2 * i + k // 4 + 1)
                    last = pe.matmul(o[:, :], xT[:, a * K + k, bass.ds(t * P, P)], w16[i][:, k, b, :],
                                     start=(at == 0), stop=(at == len(parts) - 1))
                    if at == len(parts) - 1:
                        last.then_inc(signal, 1)
                    if at + 1 in GROUP_AT[len(groups)]:
                        count_group(*groups[GROUP_AT[len(groups)].index(at + 1)])

            def kv_product(h, t, par):
                s = T * h + t
                fixed = isinstance(t, int)
                rows = LAST if fixed and t == T - 1 else P
                pe.wait_ge(S["k_relu"], s + 1)
                pe.wait_ge(S["kv_evac"], 4 if fixed and s < 2 else 2 * s + 2)
                for p in range(4):
                    last = pe.matmul(kv_acc[h][:, p * P:(p + 1) * P], v_t[par][0:rows, p * P:(p + 1) * P],
                                     k_t[par][0:rows, p * P:(p + 1) * P], start=(fixed and t == 0 and p == 0),
                                     stop=(fixed and t == T - 1), skip_group_check=True)
                last.then_inc(S["kv_done"], 1)

            pe.wait_ge(S["consts"], 1)
            transposes(0, 0)
            node_unit(0, 0, proj[0], S["kv_full"], fresh_x=True, fresh_w=True)
            transposes(1, 1)
            node_unit(0, 1, proj[1], S["kv_full"], fresh_x=True)
            pe.wait_ge(S["kv_evac"], 1)
            node_unit(1, 0, proj[0], S["kv_full"], fresh_w=True)
            transposes(2, 0)
            pe.wait_ge(S["kv_evac"], 2)
            node_unit(1, 1, proj[1], S["kv_full"])

            pe.wait_ge(S["edges_ready"], 1)
            pe.wait_ge(S["xT_hi"], 6)
            pe.wait_ge(S["xT_lo"], 6)
            for b, (c0, n) in enumerate(EB):
                pe.transpose(agg[0][0:EC, c0:c0 + n], e_dst[0:n, b, :], ident[0:n, 0:n])
                pe.transpose(agg[1][0:EC, c0:c0 + n], e_src[0:n, b, :], ident[0:n, 0:n])
                pe.transpose(tp[0][0:1, c0:c0 + n], e_min[0:n, b:b + 1], ident[0:n, 0:n])
                pe.transpose(tp[1][0:1, c0:c0 + n], e_span[0:n, b:b + 1], ident[0:n, 0:n])
            pe.wait_ge(S["bias_in"], 48)
            pe.transpose(tp[0][:, C:C + K], bq_rows, ident[0:K, 0:K]).then_inc(S["edges_T"], 1)

            def tile(h, t, par, t2):
                s = T * h + t
                fixed = isinstance(t, int)
                beside_k, beside_v = kv_halves(h, t, kv_groups(h, t, par))
                pe.wait_ge(S["kv_evac"], 2 * s - 1)
                node_unit(2 * h, t, proj[0], S["kv_full"], beside_k, fresh_x=(h == 0), fresh_w=(h == 1 and fixed and t == 0))
                if fixed and s == 2:
                    kv_product(0, 0, 0)
                if fixed and t == 0:
                    kv_product(0, T - 1, 1)
                else:
                    kv_product(h, t - 1, 1 - par)
                if h == 0 and not (fixed and t == T - 1):
                    if fixed and t == 2:
                        pe.wait_ge(S["columns"], 5)
                    transposes(t + 1, 1 - par)
                pe.wait_ge(S["kv_evac"], 2 * s)
                node_unit(2 * h + 1, t, proj[1], S["kv_full"], beside_v, fresh_w=(h == 1 and fixed and t == 0))

            kv_tiles(pe, tile)

            def q_blocks(c, q):
                t0, n = QCH[c]
                for j in range(4):
                    if isinstance(q, int) and (c, q, j) == (0, 0, 1):
                        pe.wait_ge(S["kv_evac"], 4 * T)
                    pe.wait_ge(S["q_lo"], K * c + 4 * q + j + 1)
                    groups = q_groups(c, q, j) if c < 2 else []
                    for k in range(K):
                        for a, b in ((0, 0), (1, 0), (0, 1)):
                            w_q = w16_q[:, bass.ds(2 * K * q + 2 * k + b, 1), j * P:(j + 1) * P]
                            last = pe.matmul(proj[j % 2][:, 0:n * P], w_q.rearrange("p a n -> p (a n)"),
                                             xT[:, a * K + k, t0 * P:(t0 + n) * P],
                                             start=(k == 0 and a == b), stop=(k == K - 1 and b == 1))
                        if k == K - 1:
                            last.then_inc(S["q_full"], 1)
                            if isinstance(q, int) and (c, q, j) == (0, 0, 0):
                                kv_product(1, T - 1, 1)
                        if k in (2, 5, 7):
                            for g, i in groups[k // 3:k // 3 + 1]:
                                count_group(g, i)

            pe.wait_ge(S["kv_evac"], 4 * T - 1)
            pe.wait_ge(S["w_lo"], 12)
            q_blocks(0, 0)
            q_blocks(0, 1)
            with pe.Fori(0, 2) as q:
                q_blocks(1, q)
            q_blocks(2, 0)

            pe.wait_ge(S["adj_added"], CP)
            span = pe.value_load(flags[0:1, 0:1], min_val=0, max_val=N)
            with pe.If(span >= W):
                with pe.Fori(1, WINDOWS) as k:
                    with pe.Fori(0, C) as c:
                        pe.wait_ge(SE["e_hot"], 2 * ((k - 1) * C + c) + 2)
                        pe.matmul(agg[0][:, 0:WC], hot_src[0:EC, 0, 0, :], hot_dst[0:EC, 0, 0, :], start=True,
                                  stop=True).then_inc(SE["e_mm"], 1)
            q_blocks(2, 1)

            def g_tile(h, t, par):
                if not (isinstance(t, int) and h == 0):
                    pe.wait_ge(S["h_lo"], T * h + t - 1)
                node_unit(6 + h, t, proj[par], S["g_full"])

            pe.wait_ge(S["w_lo"], 14)
            pe.wait_ge(S["q_lo"], 3 * K + 1)
            g_tile(0, 0, 0)
            pe.wait_ge(SM["sources"], 1)
            for n in range(T):
                last = pe.matmul(agg[0][:, n:n + 1], sources[:, n * P:(n + 1) * P], ones, start=True, stop=True,
                                 skip_group_check=True)
            last.then_inc(SM["deg_full"], 1)
            pe.wait_ge(SM["max_col"], 1)
            pe.transpose(agg[1][0:1, 0:P], m_col, ident[:, :]).then_inc(SM["max_T"], 1)
            pe.wait_ge(S["q_lo"], 3 * K + 2)
            g_tile(0, 1, 1)
            pe.wait_ge(S["w_lo"], 16)
            for h in range(2):
                with pe.Fori(1 - h, T // 2) as t2:
                    for par in range(2):
                        g_tile(h, 2 * t2 + par, par)

            pe.wait_ge(SM["kvs"], 4)
            for n in range(2):
                pe.wait_ge(SM[f"wo_in{n}"], 16)
                for p in range(PAIRS):
                    i = PAIRS * n + p
                    if i >= 4:
                        pe.wait_ge(SM["m_lo"], i - 3)
                    elif i == 2:
                        pe.wait_ge(S["h_lo"], 2 * T)
                    pe.matmul(m_bank[i % 4][:, :], kvs[:, p, :], wo[n][:, p, :], start=True,
                              stop=True).then_inc(SM["prod_full"], 1)

            def piece(i):
                kind, a, b = pieces[i]
                o = tp[i % 2][:, :].bitcast(BF16)
                pe.wait_ge(SF["w16_ready"], i + 1)
                if i >= 2:
                    pe.wait_ge(SF["wT_moved"], sum(moves_of[:i - 1]))
                if kind == "gu":
                    n = FR[b]
                    for k in range(K):
                        last = pe.transpose(o[:, k * P:k * P + n], raw16[i % 2][0:n, k * P:(k + 1) * P], ident16[0:n, 0:n])
                else:
                    for j in range(FB):
                        n = FR[j]
                        for k in range(2):
                            last = pe.transpose(o[0:n, (2 * j + k) * P:(2 * j + k + 1) * P],
                                                raw16[i % 2][:, k * FF + j * P:k * FF + j * P + n], ident16[:, :])
                last.then_inc(SF["wT_full"], 1)
                if kind == "down":
                    for k in range(2):
                        kk = a + k
                        pe.wait_ge(SF["diag"], kk + 1)
                        pe.matmul(kv_acc[kk // 4][:, (kk % 4) * P:(kk % 4 + 1) * P], ones_m, diag[:, kk % 4, :],
                                  start=(kk % 4 == 0), stop=True, skip_group_check=True).then_inc(SF["drow_full"], 1)

            agg_matmuls = [(s, b) for s in range(T) for b in range(2)]

            def tile_b(t, par, t2):
                fixed = isinstance(t, int)

                def beside(product):
                    if fixed and (t, product) in pe_slots:
                        piece(pe_slots.index((t, product)))

                def aggregate(n, fresh):
                    for s, b in agg_matmuls:
                        last = pe.matmul(agg[n][:, :], a_t[par][:, s, :], h16[:, s, b * D + n * HALF:b * D + (n + 1) * HALF],
                                         start=(fresh and s == 0 and b == 0), stop=(s == T - 1 and b == 1),
                                         skip_group_check=True)
                    return last

                pe.wait_ge(SB["a_ready"], t + 1)
                for n in range(2):
                    if not (fixed and t == 0):
                        pe.wait_ge(SB["agg_moved"], 2 * t - 1 + n)
                    aggregate(n, True).then_inc(SB["agg_full"], 1)
                with pe.If(most > COUNT_MAX):
                    with pe.Fori(0, ROUNDS - 1) as r:
                        pe.wait_ge(SB["a_more"], t * (ROUNDS - 1) + r + 1)
                        aggregate(0, False)
                        aggregate(1, False).then_inc(SB["a_more_used"], 1)
                beside(0)
                beside(1)
                for n in range(2):
                    if fixed and t == 0:
                        pe.wait_ge(SM["m_lo"], 2 * PAIRS)
                    else:
                        pe.wait_ge(SB["mix_moved"], 2 * t - 1 + n)
                    for k in range(K):
                        for a, b in ((0, 0), (0, 1), (1, 0)):
                            q_k = qT[:, bass.ds(t, 1), a * K + k, :].rearrange("p a n -> p (a n)")
                            last = pe.matmul(proj[n][:, :], q_k, m16[b][:, k, n * HALF:(n + 1) * HALF],
                                             start=(k == 0 and a == b), stop=(k == K - 1 and a == 1))
                    last.then_inc(SB["mix_full"], 1)
                    beside(2 + n)

            pe.wait_ge(SM["max_col"], 2)
            most = pe.value_load(flags[0:1, 1:2], min_val=0, max_val=E + 1)
            over_tiles(pe, tile_b)
            def broadcast(i, b):
                pe.wait_ge(SC["m_ready"], i + 1)
                pe.transpose(bank[b][0:1, 0:P], m_col, ident[:, :]).then_inc(SC["m_T"], 1)
                pe.wait_ge(SC["s_row"], i + 1)
                pe.matmul(bank[b + 1][:, 0:1], ones_r[:, :], row[:, 6:7], start=True, stop=True).then_inc(SC["s_bc"], 1)

            broadcast(0, 6)

            def xq_tile(t):
                o = tp[t % 2][:, :].bitcast(BF16)
                pe.wait_ge(SC["q_ready"], t + 1)
                if t >= 2:
                    pe.wait_ge(SC["qT_moved"], t - 1)
                for k in range(K):
                    last = pe.transpose(o[:, k * P:(k + 1) * P], q16[t % 2][:, k * P:(k + 1) * P], ident16[:, :])
                last.then_inc(SC["qT_full"], 1)

            def gate_up(u):
                c, b = UNIT[u]
                (c0, w), n = NCH[c], FR[b]
                pair = (bank[0:2], bank[6:8])[u % 2]
                pe.wait_ge(SC["qT_moved"], (c0 + w) // P)
                if u >= 2:
                    pe.wait_ge(SC["silu"], u - 1)
                    pe.wait_ge(SC["up_moved"], u - 1)
                for m in range(2):
                    for k in range(K):
                        last = pe.matmul(pair[m][0:n, 0:w], wguT[:, 2 * k + m, b * P:b * P + n],
                                         xqT[:, k, c0:c0 + w], start=(k == 0), stop=(k == K - 1))
                    last.then_inc(SC["gate_full"], 1)

            pe.wait_ge(SF["wT_moved"], sum(moves_of))
            for what, i in PE_FFN:
                xq_tile(i) if what == "q" else gate_up(i)
            broadcast(1, 6)

            def y_tile(t, par, first=False):
                for n in range(2):
                    if not first:
                        pe.wait_ge(SC["y_moved"], 2 * t + n - 3)
                    for b in range(FB):
                        r = FR[b]
                        last = pe.matmul(bank[2 * par + n + (4 if par else 0)][:, :], hq[0:r, b, bass.ds(t * P, P)],
                                         wdT[0:r, b, n * HALF:(n + 1) * HALF], start=(b == 0), stop=(b == FB - 1))
                    last.then_inc(SC["y_full"], 1)

            pe.wait_ge(SC["hq"], 2)
            y_tile(0, 0, True)
            pe.wait_ge(SC["hq"], 4)
            y_tile(1, 1, True)
            y_tile(2, 0)
            y_tile(3, 1)
            pe.wait_ge(SC["hq"], 6)
            with pe.Fori(2, 4) as t2:
                for par in range(2):
                    y_tile(2 * t2 + par, par)
            pe.wait_ge(SC["hq"], 8)
            for t in (8, 9):
                y_tile(t, t % 2)


        @block.scalar
        def _(act):
            def xT_high(t):
                for j in range(2):
                    act.wait_ge(S["xT_full"], 2 * t + j + 1)
                    act.wait_ge(S["consts"], 1)
                    act.activation(xT[:, 4 * j:4 * j + 4, bass.ds(t * P, P)], tp[j][:, :].rearrange("p (k n) -> p k n", n=P),
                                   ACT.Copy, scale=X_UP).then_inc(S["xT_hi"], 1)

            def weight_high(i, c):
                act.wait_ge(S[f"w_in{i}_{c}"], 16)
                if i == 2:
                    act.wait_ge(S["w_lo"], 4)
                elif i >= 4:
                    act.wait_ge(S["kv_full"], 4 * T if i >= 6 else 2 * T)
                act.activation(w16[i][:, 4 * c:4 * c + 4, 0, :], w_raw[i][:, 4 * c:4 * c + 4, :], ACT.Copy,
                               scale=W_UP).then_inc(S["w_hi"], 1)

            def relu_k(s, par):
                act.wait_ge(S["kv_evac"], s + 1 if isinstance(s, int) and s < 2 else 2 * s + 1)
                act.activation(k_t[par], k_t[par], ACT.Relu).then_inc(S["k_relu"], 1)

            weight_high(0, 0)
            xT_high(0)
            weight_high(0, 1)
            weight_high(1, 0)
            xT_high(1)
            weight_high(1, 1)
            relu_k(0, 0)
            relu_k(1, 1)
            xT_high(2)

            def tile(h, t, par, t2):
                fixed = isinstance(t, int)
                i = weights_beside(h, t)
                relu_k(T * h + t, par)
                if h == 0 and not (fixed and t == T - 1):
                    xT_high(t + 1)
                if i:
                    weight_high(i, 0)
                    weight_high(i, 1)

            kv_tiles(act, tile)

            act.wait_ge(S["kv_done"], 2 * T)
            for c, (t0, n) in enumerate(QCH):
                for m in range(K):
                    o = proj[m % 2][:, 0:n * P]
                    act.wait_ge(S["q_full"], K * c + m + 1)
                    act.activation(o, o, ACT.Relu, bias=bq_c[:, m:m + 1], scale=1.0 / (X_UP * W_UP)).then_inc(S["q_relu"], 1)
                    act.wait_ge(S["q_relu"], K * c + m + 1)
                    act.activation(qT[:, t0:t0 + n, m, :], o.rearrange("p (t n) -> p t n", n=P),
                                   ACT.Copy).then_inc(S["q_hi"], 1)
                    for i in WEIGHTS_AFTER.get((c, m), ()):
                        weight_high(*i)
            act.wait_ge(SC["clip_in"], 32)
            act.activation(row[:, 2:4], row[:, 0:2], ACT.Exp, scale=-1.0).then_inc(SC["exp"], 1)

            for h in range(2):
                with act.Fori(0, T // 2) as t2:
                    for par in range(2):
                        t = 2 * t2 + par
                        act.wait_ge(S["g_full"], T * h + t + 1)
                        act.wait_ge(SM["dinv"], 3)
                        act.activation(h16[:, bass.ds(t, 1), h * HALF:(h + 1) * HALF].rearrange("p a n -> p (a n)"),
                                       proj[par][:, :], ACT.Copy, scale=dinv_up[:, bass.ds(t, 1)]).then_inc(S["h_hi"], 1)

            for i in range(2 * PAIRS):
                n, p = i // PAIRS, i % PAIRS
                act.wait_ge(SM["prod_full"], i + 1)
                act.activation(m16[0][:, p, n * HALF:(n + 1) * HALF], m_bank[i % 4][:, :], ACT.Copy).then_inc(SM["m_hi"], 1)

            act.wait_ge(SC["c_step"], 1)

            def piece16(i):
                rows, columns = (FR[pieces[i][2]], D) if pieces[i][0] == "gu" else (P, 2 * FF)
                act.wait_ge(SF["wq_ready"], i + 1)
                if i >= 2:
                    act.wait_ge(SF["wT_full"], i - 1)
                act.activation(raw16[i % 2][0:rows, 0:columns], raw[i % 2][0:rows, 0:columns], ACT.Identity,
                               bias=neg_magic[0:rows]).then_inc(SF["w16_ready"], 1)

            piece16(0)
            for i, (kind, a, b) in enumerate(pieces):
                if i + 1 < len(pieces):
                    piece16(i + 1)
                act.wait_ge(SF["wT_full"], i + 1)
                o = tp[i % 2][:, :].bitcast(BF16).rearrange("p (k n) -> p k n", n=P)
                if kind == "gu":
                    n = FR[b]
                    act.activation(wguT.rearrange("p (k m) f -> p k m f", m=2)[:, :, a, b * P:b * P + n], o[:, :, 0:n],
                                   ACT.Copy).then_inc(SF["wT_moved"], 1)
                else:
                    for j0, j1 in ((0, FB - 1), (FB - 1, FB)):
                        n = FR[j0]
                        act.activation(wdT[0:n, j0:j1, a * P:(a + 2) * P],
                                       o[0:n, 2 * j0:2 * j1, :].rearrange("p (j k) n -> p j (k n)", k=2),
                                       ACT.Copy).then_inc(SF["wT_moved"], 1)

            def affine(t):
                if t >= 2:
                    act.wait_ge(SC["q_ready"], t - 1)
                act.activation(q_c[1], x2[:, t, :], ACT.Identity, bias=xn_shift[:, t:t + 1],
                               scale=xn_scale[:, t:t + 1]).then_inc(SC["affine"], 1)

            def xq_tile(t):
                act.wait_ge(SC["qT_full"], t + 1)
                act.activation(xqT[:, :, t * P:(t + 1) * P],
                               tp[t % 2][:, :].bitcast(BF16).rearrange("p (k n) -> p k n", n=P),
                               ACT.Copy).then_inc(SC["qT_moved"], 1)
                if t in AFFINE_AFTER:
                    affine(AFFINE_AFTER[t])

            def silu(u):
                c, b = UNIT[u]
                w, n = NCH[c][1], FR[b]
                act.wait_ge(SC["gate_full"], 2 * u + 1)
                if u >= 2:
                    act.wait_ge(SC["up_moved"], u - 1)
                act.activation(sg[0:n, u % 2, 0:w], (bank[0], bank[6])[u % 2][0:n, 0:w], ACT.Silu,
                               scale=gus[0:n, b:b + 1]).then_inc(SC["silu"], 1)

            act.wait_ge(SC["xn_columns"], 1)
            affine(1)
            for what, i in ACT_FFN:
                xq_tile(i) if what == "q" else silu(i)
            for i, (c0, w, b0, nb) in enumerate(HQ_PARTS):
                n = FR[b0]
                act.wait_ge(SC["h_rounded"], i + 1)
                act.activation(hq[0:n, b0:b0 + nb, c0:c0 + w], hT[0:n, b0:b0 + nb, c0:c0 + w], ACT.Identity,
                               bias=neg_magic[0:n]).then_inc(SC["hq"], 1)


        @block.vector
        def _(dve):
            steps = [0]

            def step(ins):
                steps[0] += 1
                ins.then_inc(S["dve_step"], 1)
                dve.wait_ge(S["dve_step"], steps[0])

            def deviation(n, par, n2):
                x_n = x_in[par]
                dve.wait_ge(S[f"x_in{par}"], 16 * n2 + 16)
                for h in range(2):
                    dve.bn_stats(stats[:, h, :], x_n[:, h * HALF:(h + 1) * HALF]).then_inc(S["ln_step"], 1)
                dve.drain()
                dve.bn_aggr(mv, stats[:, :, :].rearrange("p a b -> p (a b)")).then_inc(S["ln_step"], 1)
                dve.wait_ge(S["ln_step"], 3 * n + 3)
                dve.tensor_scalar(var_eps, mv[:, 1:2], EPS, None, ALU.add).then_inc(S["var_ready"], 1)

            def normalise(n, par):
                dve.wait_ge(S["rstd_ready"], n + 1)
                dve.tensor_scalar(x_in[par], x_in[par], mv[:, 0:1], rstd, ALU.subtract, ALU.mult).then_inc(S["ln_done"], 1)

            def layernorm(n, par, n2):
                deviation(n, par, n2)
                normalise(n, par)

            def xT_low(t):
                for j in range(2):
                    dve.wait_ge(S["xT_hi"], 2 * t + j + 1)
                    high, low = [xT[:, a * K + 4 * j:a * K + 4 * j + 4, bass.ds(t * P, P)] for a in range(2)]
                    dve.scalar_tensor_tensor(low, tp[j][:, :].rearrange("p (k n) -> p k n", n=P), X_UP, high, ALU.mult,
                                             ALU.subtract).then_inc(S["xT_lo"], 1)

            def weight_low(i, c):
                dve.wait_ge(S["w_hi"], 2 * i + 1 + c)
                s = slice(4 * c, 4 * c + 4)
                dve.scalar_tensor_tensor(w16[i][:, s, 1, :], w_raw[i][:, s, :], W_UP, w16[i][:, s, 0, :], ALU.mult,
                                         ALU.subtract).then_inc(S["w_lo"], 1)

            def kv_evac(h, t, j, par):
                s = T * h + t
                o, b = ((k_t, bk_b), (v_t, bv_b))[j]
                if isinstance(t, int) and s < 2:
                    dve.wait_ge(S["kv_full"], 2 * j + s + 1)
                    dve.wait_ge(S["bias_in"], 48)
                    acc = proj[s]
                else:
                    if j == 0:
                        dve.wait_ge(S["kv_done"], s - 1)
                    dve.wait_ge(S["kv_full"], 2 * s + j + 1)
                    acc = proj[j]
                dve.scalar_tensor_tensor(o[par], acc[:, :], 1.0 / (X_UP * W_UP), b[:, h * HALF:(h + 1) * HALF],
                                         ALU.mult, ALU.add).then_inc(S["kv_evac"], 1)

            for e in (e_dst, e_src):
                dve.memset(e[EB[2][1]:P, 2, :], 0.0).then_inc(S["scratch_set"], 1)
            step(dve.memset(cols[:, :], 0.0))
            for c, value in ((neg_magic, -MAGIC), (ones, 1.0), (exponent, -0.5), (half_neg, -0.5)):
                step(dve.memset(c, value))
            step(dve.memset(ones_r[:, :], 1.0))
            step(dve.memset(keyT[:, C:], -1.0))
            step(dve.memset(loT[:, C:], 0.0))
            step(dve.memset(base_row[:, C:], 0))
            dve.nop().then_inc(SC["c_step"], 1)
            dve.nop().then_inc(S["q_lo"], 2)
            dve.nop().then_inc(SB["a_more_used"], 1)
            layernorm(0, 0, 0)
            xT_low(0)
            weight_low(0, 0)
            layernorm(1, 1, 0)
            weight_low(0, 1)
            xT_low(1)
            kv_evac(0, 0, 0, 0)
            weight_low(1, 0)
            weight_low(1, 1)
            layernorm(2, 0, 1)
            kv_evac(0, 1, 0, 1)
            dve.wait_ge(S["edges_in"], 64)
            dst_i, src_i, tile_i = e_dst.bitcast(I32), e_src.bitcast(I32), e_tmp.bitcast(I32)
            lowest = e_min[:, 0:3].rearrange("p (b a) -> p b a", a=1).broadcast_to([P, 3, EC])
            step(dve.tensor_reduce(e_min[:, 0:3], dst_i, AX.X, ALU.min))
            step(dve.tensor_reduce(e_span[:, 0:3], dst_i, AX.X, ALU.max))
            step(dve.tensor_tensor(e_span[:, 0:3], e_span[:, 0:3], e_min[:, 0:3], ALU.subtract))
            step(dve.tensor_tensor(e_dst, dst_i, lowest, ALU.subtract))
            step(dve.tensor_scalar(tile_i, src_i, 7, None, ALU.logical_shift_right))
            step(dve.scalar_tensor_tensor(e_dst, e_dst, float(T), tile_i, ALU.mult, ALU.add))
            step(dve.tensor_scalar(tile_i, src_i, P - 1, None, ALU.bitwise_and))
            step(dve.tensor_copy(e_src, tile_i))
            dve.nop().then_inc(S["edges_ready"], 1)
            kv_evac(0, 0, 1, 0)
            xT_low(2)
            layernorm(3, 1, 1)
            dve.wait_ge(S["counts_set"], 1)
            dve.wait_ge(S["consts"], 3)
            by_node = counts[:, :].rearrange("p (n s) -> p n s", s=T)
            for t in range(T):
                r = P if t < T - 1 else LAST
                step(dve.tensor_copy(by_node[:, t * P:t * P + r, t], ident[:, 0:r]))
            step(dve.tensor_copy(ident16[:, :], ident[:, :]))
            kv_evac(0, 1, 1, 1)
            dve.wait_ge(S["edges_T"], 1)
            dve.tensor_scalar(base_row[:, 0:C], tp[0][0:1, 0:C], float(T), float((N - 1) * T), ALU.mult,
                              ALU.min).then_inc(S["columns"], 1)
            dve.tensor_copy(loT[0:EC, 0:C], agg[1][0:EC, 0:C]).then_inc(S["columns"], 1)
            dve.tensor_copy(keyT[0:EC, 0:C], agg[0][0:EC, 0:C]).then_inc(S["columns"], 1)
            dve.tensor_copy(bq_c[:, :], tp[0][:, C:C + K]).then_inc(S["columns"], 1)
            dve.tensor_reduce(flags[:, 0:1], tp[1][0:1, 0:C], AX.X, ALU.max).then_inc(S["columns"], 1)
            dve.wait_ge(S["columns"], 5)

            def one_hot_dst(g, i):
                key = keyT[0:EC, bass.ds(g * G, G)].rearrange("p (g a) -> p g a", a=1).broadcast_to([EC, G, WC])
                dve.tensor_tensor(hot_dst[0:EC, i], iota_w[0:EC], key, ALU.is_equal).then_inc(S["hot_dst_ready"], 1)

            def count(g, i):
                dve.wait_ge(S["adj_mm"], g + 1)
                _, starts = nc.values_load_multi_w_load_instructions(
                    base_row[0:1, bass.ds(g * G, G)], engines=[mybir.EngineType.DVE], min_val=0, max_val=(N - 1) * T,
                    skip_runtime_bounds_check_because="base_row is clamped to these bounds")
                for k in range(G):
                    c, at = g * G + k, starts[k]
                    if not (isinstance(c, int) and c == 0):
                        dve.wait_ge(S["adj_added"], c)
                    window = counts[:, bass.ds(at, WC)]
                    dve.tensor_tensor(window, agg[i][:, k * WC:(k + 1) * WC], window,
                                      ALU.add).then_inc(S["adj_added"], 1)
                one_hot_dst(g + 2, i)

            one_hot_dst(0, 0)
            one_hot_dst(1, 1)

            def tile(h, t, par, t2):
                fixed = isinstance(t, int)
                beside_k, beside_v = kv_halves(h, t, kv_groups(h, t, par))
                i = weights_beside(h, t)
                ahead = h == 0 and not (fixed and t >= T - 2)
                if ahead:
                    deviation(t + 2, par, t2 + 1)
                for g in beside_k[:-1]:
                    count(*g)
                if ahead:
                    normalise(t + 2, par)
                kv_evac(h, t, 0, par)
                for g in beside_k[-1:]:
                    count(*g)
                if h == 0 and not (fixed and t == T - 1):
                    xT_low(t + 1)
                if i:
                    weight_low(i, 0)
                for g in beside_v[:-1]:
                    count(*g)
                kv_evac(h, t, 1, par)
                count(*beside_v[-1])
                if i:
                    weight_low(i, 1)

            kv_tiles(dve, tile)

            def q_low(c, m, acc):
                t0, n = QCH[c]
                dve.wait_ge(S["q_hi"], K * c + m + 1)
                high, low = [qT[:, t0:t0 + n, bass.ds(m + a * K, 1), :] for a in range(2)]
                dve.tensor_tensor(low, acc[:, 0:n * P].rearrange("p (t a n) -> p t a n", a=1, n=P), high,
                                  ALU.subtract).then_inc(S["q_lo"], 1)

            for c in range(2):
                with dve.Fori(0, 2) as q:
                    for j in range(4):
                        for g, i in q_groups(c, q, j):
                            count(g, i)
                        q_low(c, 4 * q + j, proj[j % 2])
                for i in LOWS_AFTER.get((c, K - 1), ()):
                    weight_low(*i)
            for m in range(4):
                q_low(2, m, proj[m % 2])
                for i in LOWS_AFTER.get((2, m), ()):
                    weight_low(*i)

            dve.wait_ge(S["adj_added"], CP)
            dve.wait_ge(S["hot_src_ready"], G * (GROUPS + 2))
            span = dve.value_load(flags[0:1, 0:1], min_val=0, max_val=N)
            with dve.If(span >= W):
                with dve.Fori(1, WINDOWS) as k:
                    dve.drain()
                    dve.tensor_scalar(keyT[0:EC, :], keyT[0:EC, :], float(-WC), None, ALU.add)
                    dve.tensor_scalar(base_row[:, :], base_row[:, :], float(WC), float(N * T), ALU.add, ALU.min)
                    dve.drain()
                    with dve.Fori(0, C) as c:
                        dve.tensor_scalar(hot_dst[0:EC, 0, 0, :], iota_w[0:EC, 0, :], keyT[0:EC, bass.ds(c, 1)],
                                          None, ALU.is_equal).then_inc(SE["e_hot"], 1)
                        dve.tensor_scalar(hot_src[0:EC, 0, 0, :], iota_p[0:EC, :], loT[0:EC, bass.ds(c, 1)],
                                          None, ALU.is_equal).then_inc(SE["e_hot"], 1)
                        at = dve.value_load(base_row[0:1, bass.ds(c, 1)], min_val=0, max_val=N * T)
                        window = counts[:, bass.ds(at, WC)]
                        dve.wait_ge(SE["e_mm"], (k - 1) * C + c + 1)
                        dve.tensor_tensor(window, agg[0][:, 0:WC], window, ALU.add)
                        dve.drain()

            NS = NP // 4
            dve.wait_ge(S["w_lo"], 16)
            for j in range(4):
                dve.tensor_reduce(sources[:, j * NS:(j + 1) * NS], by_node[:, j * NS:(j + 1) * NS, :], AX.X,
                                  ALU.add).then_inc(S["dve_step"], 1)
                steps[0] += 1
                q_low(2, 4 + j, proj[j % 2])
            dve.wait_ge(S["dve_step"], steps[0])
            dve.nop().then_inc(SM["sources"], 1)
            step(dve.tensor_reduce(m_col, sources, AX.X, ALU.max))
            dve.nop().then_inc(SM["max_col"], 1)
            dve.wait_ge(SM["deg_full"], 1)
            dve.tensor_scalar(dinv, agg[0][:, 0:T], 1.0, None, ALU.max).then_inc(SM["deg_ready"], 1)
            dve.wait_ge(SM["max_T"], 1)
            dve.tensor_reduce(flags[:, 1:2], agg[1][0:1, 0:P], AX.X, ALU.max).then_inc(SM["max_col"], 1)
            dve.wait_ge(SC["exp"], 1)
            step(dve.tensor_scalar(row[:, 4:6], row[:, 2:4], 1.0, QMAX, ALU.add, ALU.mult))
            step(dve.reciprocal(row[:, 4:6], row[:, 4:6]))
            step(dve.memset(kvs, 0.0))
            dve.wait_ge(S["kv_done"], 2 * T)
            for b in range(2):
                acc = kv_acc[b][:, :].rearrange("p (q n) -> p q n", n=P)
                for h in range(2):
                    r = slice(h * DH, (h + 1) * DH)
                    dve.tensor_scalar(kvs[r, 4 * b:4 * b + 4, r], acc[r, :, r], M_UP / (N * DH), None,
                                      ALU.mult).then_inc(SM["kvs"], 1)

            def counts_tile(t):
                return counts[:, bass.ds(t * P * T, P * T)].rearrange("p (n s) -> p s n", s=T)

            def a_tile(t, par):
                dve.tensor_scalar(a_t[par], counts_tile(t), float(COUNT_MAX), None, ALU.min).then_inc(SB["a_ready"], 1)

            for h in range(2):
                with dve.Fori(0, T // 2) as t2:
                    for par in range(2):
                        t = 2 * t2 + par
                        dve.wait_ge(S["h_hi"], T * h + t + 1)
                        high, low = [h16[:, bass.ds(t, 1), a * D + h * HALF:a * D + (h + 1) * HALF].rearrange("p a n -> p (a n)")
                                     for a in range(2)]
                        dve.scalar_tensor_tensor(low, proj[par][:, :], dinv_up[:, bass.ds(t, 1)], high, ALU.mult,
                                                 ALU.subtract).then_inc(S["h_lo"], 1)

            for i in range(2 * PAIRS):
                n, p = i // PAIRS, i % PAIRS
                dve.wait_ge(SM["m_hi"], i + 1)
                s = slice(n * HALF, (n + 1) * HALF)
                dve.tensor_tensor(m16[1][:, p, s], m_bank[i % 4][:, :], m16[0][:, p, s], ALU.subtract).then_inc(SM["m_lo"], 1)
                if i == 1:
                    a_tile(0, 0)
            dve.wait_ge(SM["prod_full"], 2 * PAIRS)
            step(dve.memset(ones_m, 1.0))
            dve.wait_ge(SM["gb_in"], 16)
            dve.wait_ge(SM["max_col"], 2)
            most = dve.value_load(flags[0:1, 1:2], min_val=0, max_val=E + 1)

            def weight_scale(i, w, n):
                step(dve.tensor_reduce(wsc[0:n, i:i + 1], w, AX.X, ALU.max, apply_absolute_value=True))
                step(dve.tensor_scalar(wsc[0:n, i:i + 1], wsc[0:n, i:i + 1], 1.0 / QMAX, None, ALU.mult))
                step(dve.reciprocal(wrc[0:n, i:i + 1], wsc[0:n, i:i + 1]))
                step(dve.tensor_scalar(w, w, wrc[0:n, i:i + 1], MAGIC, ALU.mult, ALU.add))
                step(dve.tensor_scalar(w, w, MAGIC + QMAX, MAGIC - QMAX - 1.0, ALU.min, ALU.max))

            def piece(i):
                kind, a, b = pieces[i]
                dve.wait_ge(SF[f"raw_in{i % 2}"], 16 * (i // 2 + 1))
                if kind == "gu":
                    weight_scale(FB * a + b, raw[i % 2][0:FR[b], :], FR[b])
                else:
                    for k in range(2):
                        kk = a + k
                        weight_scale(2 * FB + kk, raw[i % 2][:, k * FF:(k + 1) * FF], P)
                        if kk >= 4:
                            dve.wait_ge(SF["drow_full"], kk - 3)
                        dve.tensor_scalar(diag[:, kk % 4, :], ident[:, :], wsc[:, 2 * FB + kk:2 * FB + kk + 1], None,
                                          ALU.mult).then_inc(SF["diag"], 1)
                dve.nop().then_inc(SF["wq_ready"], 1)

            def tile_b(t, par, t2):
                fixed = isinstance(t, int)
                last_tile = fixed and t == T - 1
                rows = LAST if last_tile else P
                row_x2 = x2[:, bass.ds(t, 1), :].rearrange("p a d -> p (a d)")

                def beside(product):
                    if fixed and (t, product) in slots:
                        piece(slots.index((t, product)))

                if not last_tile:
                    a_tile(t + 1, 1 - par)
                beside(0)
                with dve.If(most > COUNT_MAX):
                    with dve.Fori(0, ROUNDS - 1) as r:
                        dve.wait_ge(SB["agg_full"], 2 * t + 2)
                        dve.wait_ge(SB["a_more_used"], t * (ROUNDS - 1) + r + 1)
                        dve.tensor_scalar(counts_tile(t), counts_tile(t), float(-COUNT_MAX), 0.0, ALU.add, ALU.max)
                        dve.drain()
                        dve.tensor_scalar(a_t[par], counts_tile(t), float(COUNT_MAX), None, ALU.min).then_inc(SB["a_more"], 1)
                    dve.wait_ge(SB["a_more_used"], (t + 1) * (ROUNDS - 1) + 1)
                    dve.memset(stats[:, 0, 0:1], 0.0)
                beside(1)
                dve.wait_ge(SB["x_bias"], t + 1)
                for n in range(2):
                    s = slice(n * HALF, (n + 1) * HALF)
                    dve.wait_ge(SB["agg_full"], 2 * t + n + 1)
                    dve.scalar_tensor_tensor(agg[n][:, :], agg[n][:, :], dinv_down[:, bass.ds(t, 1)], gb_b[:, s],
                                             ALU.mult, ALU.add)
                    dve.drain()
                    dve.scalar_tensor_tensor(x_t[par][:, s], agg[n][:, :], 0.0, x_t[par][:, s], ALU.max,
                                             ALU.add).then_inc(SB["agg_moved"], 1)
                for n in range(2):
                    s = slice(n * HALF, (n + 1) * HALF)
                    beside(2 + n)
                    dve.drain()
                    dve.wait_ge(SB["mix_full"], 2 * t + n + 1)
                    dve.scalar_tensor_tensor(row_x2[:, s], proj[n][:, :], 1.0 / M_UP, x_t[par][:, s], ALU.mult,
                                             ALU.add).then_inc(SB["mix_moved"], 1)
                    dve.drain()
                    dve.bn_stats(stats[:, n, :], row_x2[:, s])
                    for top, op in ((x_top, ALU.max), (x_low, ALU.min)):
                        dve.tensor_reduce(top[0:rows, n:n + 1], row_x2[0:rows, s], AX.X, op)
                dve.drain()
                dve.bn_aggr(mv, stats[:, :, :].rearrange("p a b -> p (a b)"))
                dve.drain()
                dve.tensor_scalar(var_eps, mv[:, 1:2], EPS, None, ALU.add).then_inc(SB["b_var"], 1)
                dve.tensor_tensor(x_ends[:, 0:1], x_top[:, 0:1], x_top[:, 1:2], ALU.max)
                dve.tensor_tensor(x_ends[:, 1:2], x_low[:, 0:1], x_low[:, 1:2], ALU.min)
                dve.tensor_copy(ln_mean[:, bass.ds(t, 1)], mv[:, 0:1])
                dve.drain()
                dve.wait_ge(SB["b_rstd"], t + 1)
                dve.tensor_scalar(x_ends, x_ends, mv[:, 0:1], rstd, ALU.subtract, ALU.mult)
                dve.tensor_copy(ln_rstd[:, bass.ds(t, 1)], rstd)
                dve.drain()
                dve.tensor_reduce(mx[0:rows, bass.ds(t, 1)], x_ends[0:rows, :], AX.X, ALU.max,
                                  apply_absolute_value=True).then_inc(SB["b_max"], 1)

            over_tiles(dve, tile_b)

            def scale(i, columns, dst, rdst):
                step(dve.tensor_reduce(m_col, columns, AX.X, ALU.max))
                dve.nop().then_inc(SC["m_ready"], 1)
                dve.wait_ge(SC["m_T"], i + 1)
                step(dve.tensor_reduce(row[:, 7:8], bank[6][0:1, 0:P], AX.X, ALU.max))
                dve.tensor_tensor(row[:, 6:7], row[:, 7:8], row[:, 4 + i:5 + i], ALU.mult).then_inc(SC["s_row"], 1)
                dve.wait_ge(SC["s_bc"], i + 1)
                step(dve.tensor_copy(dst, bank[7][:, 0:1]))
                step(dve.reciprocal(rdst, dst))

            dve.wait_ge(SB["b_max"], T)
            scale(0, mx, s_x, rs_x)
            step(dve.tensor_scalar(xn_scale, ln_rstd, rs_x, None, ALU.mult))
            step(dve.scalar_tensor_tensor(xn_shift, ln_mean, -1.0, xn_scale, ALU.mult, ALU.mult))
            dve.nop().then_inc(SC["xn_columns"], 1)
            def xq_tile(t):
                q = q_c[t % 2]
                if t % 2 == 0:
                    step(dve.tensor_scalar(q, x2[:, t, :], xn_scale[:, t:t + 1], xn_shift[:, t:t + 1], ALU.mult, ALU.add))
                else:
                    dve.wait_ge(SC["affine"], t // 2 + 1)
                step(dve.tensor_scalar(q, q, MAGIC, MAGIC + QMAX, ALU.add, ALU.min))
                if t >= 2:
                    dve.wait_ge(SC["qT_full"], t - 1)
                dve.tensor_scalar(q16[t % 2], q, MAGIC - QMAX - 1.0, -MAGIC, ALU.max, ALU.add).then_inc(SC["q_ready"], 1)

            xq_tile(0)
            step(dve.tensor_scalar(gus, wsc[:, 0:2 * FB], s_x, None, ALU.mult))

            def up(u):
                c, b = UNIT[u]
                (c0, w), n = NCH[c], FR[b]
                dve.wait_ge(SC["gate_full"], 2 * u + 2)
                dve.wait_ge(SC["silu"], u + 1)
                dve.scalar_tensor_tensor(hT[0:n, b, c0:c0 + w], (bank[1], bank[7])[u % 2][0:n, 0:w],
                                         gus[0:n, FB + b:FB + b + 1], sg[0:n, u % 2, 0:w], ALU.mult,
                                         ALU.mult).then_inc(SC["up_moved"], 1)
                dve.wait_ge(SC["up_moved"], u + 1)
                step(dve.tensor_reduce(mh[0:n, u:u + 1], hT[0:n, b, c0:min(c0 + w, N)], AX.X, ALU.max,
                                       apply_absolute_value=True))

            for what, i in DVE_FFN[1:]:
                xq_tile(i) if what == "q" else up(i)
            scale(1, mh, s_d, rs_d)
            def h_parts(parts):
                for c0, w, b0, nb in parts:
                    n = FR[b0]
                    a = hT[0:n, b0:b0 + nb, c0:c0 + w]
                    step(dve.tensor_scalar(a, a, rs_d[0:n], MAGIC, ALU.mult, ALU.add))
                    dve.tensor_scalar(a, a, MAGIC + QMAX, MAGIC - QMAX - 1.0, ALU.min, ALU.max).then_inc(SC["h_rounded"], 1)

            h_parts(HQ_PARTS[:6])
            dve.wait_ge(SF["drow_full"], K)
            for j in range(2):
                step(dve.tensor_scalar(d_row[:, j * HALF:(j + 1) * HALF], kv_acc[j][:, :], s_d, None, ALU.mult))

            def y_tile(t, par, fixed=False):
                row_x2 = x2[:, bass.ds(t, 1), 0:HALF].rearrange("p a d -> p (a d)")
                if not fixed:
                    dve.wait_ge(SC["y_ready1"], t - 1)
                for n in range(2):
                    s = slice(n * HALF, (n + 1) * HALF)
                    dve.wait_ge(SC["y_full"], 2 * t + n + 1)
                    dve.tensor_tensor(y_t[par][:, s], (bank[0:2], bank[6:8])[par][n][:, :], d_row[:, s],
                                      ALU.mult).then_inc(SC["y_moved"], 1)
                dve.wait_ge(SC["y_moved"], 2 * t + 1)
                dve.tensor_tensor(row_x2, row_x2, y_t[par][:, 0:HALF], ALU.add).then_inc(SC["y_ready0"], 1)

            y_tile(0, 0, True)
            y_tile(1, 1, True)
            h_parts(HQ_PARTS[6:])
            with dve.Fori(1, T // 2) as t2:
                y_tile(2 * t2, 0)
                y_tile(2 * t2 + 1, 1)

_INS = ['x', 'src', 'dst', 'L0_gnn_W', 'L0_gnn_b', 'L0_mix_Wq', 'L0_mix_bq', 'L0_mix_Wk', 'L0_mix_bk', 'L0_mix_Wv',
        'L0_mix_bv', 'L0_mix_Wo', 'L0_mix_bo', 'L0_ffn_clip_x', 'L0_ffn_clip_down', 'L0_ffn_w_gate', 'L0_ffn_w_up',
        'L0_ffn_w_down']


def kernel(**inputs):
    import numpy as np
    import concourse.bacc as bacc
    from concourse.bass_utils import run_bass_kernel_spmd

    nc = bacc.Bacc("TRN2", target_bir_lowering=False, num_devices=1)
    arrays, args = {}, []
    for name in _INS:
        a = np.ascontiguousarray(inputs[name])
        arrays[f"in_{name}"] = a
        args.append(nc.dram_tensor(f"in_{name}", a.shape, mybir.dt.from_np(a.dtype), kind="ExternalInput").ap())
    out = nc.dram_tensor("out_x", (N, D), F32, kind="ExternalOutput").ap()
    gps_layer(nc, *args, out)
    r = run_bass_kernel_spmd(nc, [arrays], core_ids=[0])
    return r.results[0]["out_x"]
```
